# Optimizing a Trainium2 kernel written in Bass

```python
import numpy as np
import jax
import jax.numpy as jnp

def _softmax(x, axis=-1):
    return jax.nn.softmax(x, axis=axis)

def _gelu(x):
    return jax.nn.gelu(x, approximate=True)

def _silu(x):
    return jax.nn.silu(x)

def _sigmoid(x):
    return jax.nn.sigmoid(x)

def _layernorm(x, axis=-1, eps=1e-05):
    m = jnp.mean(x, axis=axis, keepdims=True)
    v = jnp.var(x, axis=axis, keepdims=True)
    return (x - m) / jnp.sqrt(v + eps)

def _scatter_add(tgt, idx, src, axis=0):
    return tgt.at[idx].add(src)

def _segment_sum(src, seg, n):
    return jax.ops.segment_sum(src, seg, n)
kernel_name = 'mk_adaln_d4_jaxref_r8_ccca04'

def setup_inputs(seed: int=0):
    np.random.seed(seed)
    _w = jnp.asarray

    def _L0_attn_setup():
        import jax, jax.numpy as jnp
        import numpy as np
        EMB_DIM = 128
        N_HEADS = 16
        HEAD_DIM = EMB_DIM // N_HEADS
        SEQ = 256
        BSZ = 2

        def _rope_pair(q, k):
            bsz, seq_len, d_model = q.shape
            freq_range = jnp.arange(d_model // 2, dtype=jnp.float32)
            freq_cis = jnp.power(10000.0, -2.0 * freq_range / d_model)
            pos = jnp.arange(seq_len, dtype=jnp.float32)
            freq = jnp.einsum('i,j->ij', pos, freq_cis)
            sin_e = jnp.sin(freq)[None]
            cos_e = jnp.cos(freq)[None]
            q_even, q_odd = (q[..., ::2], q[..., 1::2])
            k_even, k_odd = (k[..., ::2], k[..., 1::2])
            q_rot = jnp.concatenate([q_even * cos_e - q_odd * sin_e, q_even * sin_e - q_odd * cos_e], axis=-1)
            k_rot = jnp.concatenate([k_even * cos_e - k_odd * sin_e, k_even * sin_e - k_odd * cos_e], axis=-1)
            return (q_rot, k_rot)
        key = jax.random.key(seed)
        ks = jax.random.split(key, 9)
        s = 1.0 / np.sqrt(EMB_DIM)
        return {'x': jax.random.normal(ks[0], (BSZ, SEQ, EMB_DIM), dtype=jnp.float32), 'Wq': jax.random.normal(ks[1], (EMB_DIM, EMB_DIM), dtype=jnp.float32) * s, 'bq': jax.random.normal(ks[2], (EMB_DIM,), dtype=jnp.float32) * 0.02, 'Wk': jax.random.normal(ks[3], (EMB_DIM, EMB_DIM), dtype=jnp.float32) * s, 'bk': jax.random.normal(ks[4], (EMB_DIM,), dtype=jnp.float32) * 0.02, 'Wv': jax.random.normal(ks[5], (EMB_DIM, EMB_DIM), dtype=jnp.float32) * s, 'bv': jax.random.normal(ks[6], (EMB_DIM,), dtype=jnp.float32) * 0.02, 'Wo': jax.random.normal(ks[7], (EMB_DIM, EMB_DIM), dtype=jnp.float32) * s, 'bo': jax.random.normal(ks[8], (EMB_DIM,), dtype=jnp.float32) * 0.02}
    _L0_attn_in = _L0_attn_setup()

    def _L0_ffn_setup():
        import jax, jax.numpy as jnp
        import numpy as np
        from jax import lax
        B, N, D, H, E, K = (16, 128, 128, 512, 8, 2)
        key = jax.random.key(seed)
        ks = jax.random.split(key, 12)
        s = 0.02
        return {'x': jax.random.normal(ks[0], (B, N, D), jnp.float32), 'alpha': jnp.asarray(0.9, jnp.float32), 'w_gate': jax.random.normal(ks[1], (D, E), jnp.float32) * s, 'b_gate': jnp.zeros((E,), jnp.float32), 'W1m': jax.random.normal(ks[2], (D, H), jnp.float32) * s, 'b1m': jnp.zeros((H,), jnp.float32), 'W2m': jax.random.normal(ks[3], (H, D), jnp.float32) * s, 'b2m': jnp.zeros((D,), jnp.float32), 'W1e': jax.random.normal(ks[4], (E, D, H), jnp.float32) * s, 'b1e': jnp.zeros((E, H), jnp.float32), 'W2e': jax.random.normal(ks[5], (E, H, D), jnp.float32) * s, 'b2e': jnp.zeros((E, D), jnp.float32)}
    _L0_ffn_in = _L0_ffn_setup()
    _L0_c = _w((lambda *s: np.random.randn(*s).astype(np.float32) * 0.05)(16, 128))
    _L0_wmod = _w((lambda *s: np.random.randn(*s).astype(np.float32) * 0.05)(128, 6 * 128) * 128 ** (-0.5))

    def _L1_attn_setup():
        import jax, jax.numpy as jnp
        import numpy as np
        key = jax.random.key(seed)
        k1, k2, k3 = jax.random.split(key, 3)
        B, S, D, N = (2, 256, 128, 16)
        H = D // N
        x = jax.random.normal(k1, (B, S, D), dtype=jnp.float32)
        W_qkv = jax.random.normal(k2, (N, D, 3 * H), dtype=jnp.float32) / np.sqrt(D).astype(np.float32)
        W_out = jax.random.normal(k3, (N, H, D), dtype=jnp.float32) / np.sqrt(D).astype(np.float32)
        return {'x': x, 'W_qkv': W_qkv, 'W_out': W_out}
    _L1_attn_in = _L1_attn_setup()

    def _L1_ffn_setup():
        import jax, jax.numpy as jnp
        import numpy as np
        DIM = 128
        DEPTH = 2
        HEADS = 8
        DIM_HEAD = 64
        WINDOW = 64
        INNER = HEADS * DIM_HEAD
        HID = int(DIM * 4 * 2 / 3)
        B, N = (2, 1024)
        QK_SCALE = 8.0

        def shift_token(t):
            t1, t2 = jnp.split(t, 2, axis=-1)
            t2 = jnp.pad(t2, ((0, 0), (1, 0), (0, 0)))[:, :-1]
            return jnp.concatenate([t1, t2], axis=-1)

        def l2norm(t):
            return t / jnp.clip(jnp.linalg.norm(t, axis=-1, keepdims=True), 1e-12)

        def rotate_half(x):
            x1, x2 = jnp.split(x, 2, axis=-1)
            return jnp.concatenate([-x2, x1], axis=-1)

        def rotary_xpos(q, k):
            n = q.shape[-2]
            half_idx = jnp.arange(0, DIM_HEAD, 2, dtype=jnp.float32)
            inv_freq = 1.0 / 10000.0 ** (half_idx / DIM_HEAD)
            t = jnp.arange(n, dtype=jnp.float32)
            freqs = t[:, None] * inv_freq[None, :]
            freqs = jnp.concatenate([freqs, freqs], axis=-1)
            base = (half_idx + 0.4 * DIM_HEAD) / (1.4 * DIM_HEAD)
            power = (t - n // 2) / float(WINDOW // 2)
            scale = base[None, :] ** power[:, None]
            scale = jnp.concatenate([scale, scale], axis=-1)
            cos, sin = (jnp.cos(freqs), jnp.sin(freqs))
            q = q * cos * scale + rotate_half(q) * sin * scale
            k = k * cos / scale + rotate_half(k) * sin / scale
            return (q, k)

        def local_attention(q, k, v):
            b, h, n, d = q.shape
            w = n // WINDOW
            bq = q.reshape(b, h, w, WINDOW, d) * QK_SCALE
            bk = k.reshape(b, h, w, WINDOW, d)
            bv = v.reshape(b, h, w, WINDOW, d)

            def look_around(t):
                p = jnp.pad(t, ((0, 0), (0, 0), (1, 0), (0, 0), (0, 0)))
                return jnp.concatenate([p[:, :, :w], p[:, :, 1:]], axis=3)
            bk, bv = (look_around(bk), look_around(bv))
            bt = jnp.arange(n).reshape(w, WINDOW)
            btp = jnp.pad(bt, ((1, 0), (0, 0)), constant_values=-1)
            btk = jnp.concatenate([btp[:w], btp[1:]], axis=1)
            sim = jnp.einsum('bhwid,bhwjd->bhwij', bq, bk)
            i = bt[:, :, None]
            j = btk[:, None, :]
            mask = (i < j) | (i > j + WINDOW) | (j == -1)
            sim = jnp.where(mask, -jnp.finfo(sim.dtype).max, sim)
            attn = jax.nn.softmax(sim, axis=-1)
            out = jnp.einsum('bhwij,bhwjd->bhwid', attn, bv)
            return out.reshape(b, h, n, d)

        def _layer(x, wqkv, qs, ksc, wo, lg, lb, w1, b1, w2, b2):
            b, n, _ = x.shape
            h = shift_token(x)
            qkv = h @ wqkv
            q, k, v = jnp.split(qkv, 3, axis=-1)
            to_heads = lambda t: t.reshape(b, n, HEADS, DIM_HEAD).transpose(0, 2, 1, 3)
            q, k, v = (to_heads(q), to_heads(k), to_heads(v))
            q = l2norm(q) * qs
            k = l2norm(k) * ksc
            q, k = rotary_xpos(q, k)
            o = local_attention(q, k, v)
            o = o.transpose(0, 2, 1, 3).reshape(b, n, INNER)
            x = x + o @ wo
            h = shift_token(x)
            mu = h.mean(-1, keepdims=True)
            var = h.var(-1, keepdims=True)
            h = (h - mu) / jnp.sqrt(var + 1e-05) * lg + lb
            h = h @ w1 + b1
            a, g = jnp.split(h, 2, axis=-1)
            h = a * jax.nn.gelu(g, approximate=False)
            x = x + h @ w2 + b2
            return x
        key = jax.random.key(seed)
        ks = jax.random.split(key, 6)
        return {'x': jax.random.normal(ks[0], (B, N, DIM), jnp.float32), 'wqkv': jax.random.normal(ks[1], (DEPTH, DIM, 3 * INNER), jnp.float32) * 0.02, 'q_scale': jnp.ones((DEPTH, DIM_HEAD), jnp.float32), 'k_scale': jnp.ones((DEPTH, DIM_HEAD), jnp.float32), 'wo': jax.random.normal(ks[2], (DEPTH, INNER, DIM), jnp.float32) * 0.02, 'ln_g': jnp.ones((DEPTH, DIM), jnp.float32), 'ln_b': jnp.zeros((DEPTH, DIM), jnp.float32), 'w1': jax.random.normal(ks[3], (DEPTH, DIM, 2 * HID), jnp.float32) * 0.02, 'b1': jnp.zeros((DEPTH, 2 * HID), jnp.float32), 'w2': jax.random.normal(ks[4], (DEPTH, HID, DIM), jnp.float32) * 0.02, 'b2': jnp.zeros((DEPTH, DIM), jnp.float32)}
    _L1_ffn_in = _L1_ffn_setup()
    _L1_c = _w((lambda *s: np.random.randn(*s).astype(np.float32) * 0.05)(16, 128))
    _L1_wmod = _w((lambda *s: np.random.randn(*s).astype(np.float32) * 0.05)(128, 6 * 128) * 128 ** (-0.5))

    def _L2_attn_setup():
        import jax, jax.numpy as jnp
        import numpy as np
        SEQ_LEN = 256
        DIM_EMB = 128
        DIM_K = 128
        DIM_V = 128
        key = jax.random.key(seed)
        k1, k2, k3, k4, k5 = jax.random.split(key, 5)
        scale = DIM_EMB ** (-0.5)
        return {'x': jax.random.normal(k1, (4, SEQ_LEN, DIM_EMB), dtype=jnp.float32), 'Wq': jax.random.normal(k2, (DIM_EMB, DIM_K), dtype=jnp.float32) * scale, 'Wk': jax.random.normal(k3, (DIM_EMB, DIM_K), dtype=jnp.float32) * scale, 'Wv': jax.random.normal(k4, (DIM_EMB, DIM_V), dtype=jnp.float32) * scale, 'Wo': jax.random.normal(k5, (DIM_V, DIM_V), dtype=jnp.float32) * DIM_V ** (-0.5)}
    _L2_attn_in = _L2_attn_setup()

    def _L2_ffn_setup():
        import jax, jax.numpy as jnp
        import numpy as np
        E = 128
        D = 128
        C = 32
        key = jax.random.key(seed)
        kx, kg, ke = jax.random.split(key, 3)
        x = jax.random.normal(kx, (4, 256, D), dtype=jnp.float32)
        wg = jax.random.normal(kg, (D, E), dtype=jnp.float32) * 0.02
        we = jax.random.normal(ke, (E, D, D), dtype=jnp.float32) * 0.02
        return {'x': x, 'wg': wg, 'we': we}
    _L2_ffn_in = _L2_ffn_setup()
    _L2_c = _w((lambda *s: np.random.randn(*s).astype(np.float32) * 0.05)(16, 128))
    _L2_wmod = _w((lambda *s: np.random.randn(*s).astype(np.float32) * 0.05)(128, 6 * 128) * 128 ** (-0.5))

    def _L3_attn_setup():
        import jax, jax.numpy as jnp
        import numpy as np
        H = 16
        ROPE_BASE = 10000.0

        def _rotate_half(x):
            d = x.shape[-1]
            return jnp.concatenate((-x[..., d // 2:], x[..., :d // 2]), axis=-1)
        key = jax.random.key(seed)
        ks = jax.random.split(key, 9)
        B, S, E = (4, 256, 128)
        s = 0.02
        return {'x': jax.random.normal(ks[0], (B, S, E), dtype=jnp.float32), 'wq': jax.random.normal(ks[1], (E, E), dtype=jnp.float32) * s, 'bq': jax.random.normal(ks[2], (E,), dtype=jnp.float32) * s, 'wk': jax.random.normal(ks[3], (E, E), dtype=jnp.float32) * s, 'bk': jax.random.normal(ks[4], (E,), dtype=jnp.float32) * s, 'wv': jax.random.normal(ks[5], (E, E), dtype=jnp.float32) * s, 'bv': jax.random.normal(ks[6], (E,), dtype=jnp.float32) * s, 'wo': jax.random.normal(ks[7], (E, E), dtype=jnp.float32) * s, 'bo': jax.random.normal(ks[8], (E,), dtype=jnp.float32) * s}
    _L3_attn_in = _L3_attn_setup()

    def _L3_ffn_setup():
        import jax, jax.numpy as jnp
        import numpy as np
        import math
        N_EMBD = 128
        HIDDEN = 4 * N_EMBD
        N_EXPERTS = 8
        TOP_K = 2
        B, T = (4, 256)

        def new_gelu(x):
            c = math.sqrt(2.0 / math.pi)
            return 0.5 * x * (1.0 + jnp.tanh(c * (x + 0.044715 * x * x * x)))

        def _moe_forward(x, Wfc_s, bfc_s, Wproj_s, bproj_s, Wr, Wfc, bfc, Wproj, bproj):
            Bb, Tt, C = x.shape
            xf = x.reshape(Bb * Tt, C)
            N = Bb * Tt
            shared = new_gelu(xf @ Wfc_s + bfc_s) @ Wproj_s + bproj_s
            logits = xf @ Wr
            probs = jax.nn.softmax(logits, axis=-1)
            topk_p, topk_i = jax.lax.top_k(probs, TOP_K)
            topk_p = topk_p / jnp.sum(topk_p, axis=-1, keepdims=True)
            gate = jnp.zeros((N, N_EXPERTS), dtype=xf.dtype)
            gate = gate.at[jnp.arange(N)[:, None], topk_i].add(topk_p)
            routed = jnp.zeros_like(xf)
            for e in range(N_EXPERTS):
                h = new_gelu(xf @ Wfc[e] + bfc[e]) @ Wproj[e] + bproj[e]
                routed = routed + h * gate[:, e:e + 1]
            return (shared + routed).reshape(Bb, Tt, C)
        key = jax.random.key(seed)
        ks = jax.random.split(key, 10)
        s = 0.02
        return {'x': jax.random.normal(ks[0], (B, T, N_EMBD), dtype=jnp.float32), 'Wfc_s': jax.random.normal(ks[1], (N_EMBD, HIDDEN), dtype=jnp.float32) * s, 'bfc_s': jnp.zeros((HIDDEN,), dtype=jnp.float32), 'Wproj_s': jax.random.normal(ks[2], (HIDDEN, N_EMBD), dtype=jnp.float32) * s, 'bproj_s': jnp.zeros((N_EMBD,), dtype=jnp.float32), 'Wr': jax.random.normal(ks[3], (N_EMBD, N_EXPERTS), dtype=jnp.float32) * s, 'Wfc': jax.random.normal(ks[4], (N_EXPERTS, N_EMBD, HIDDEN), dtype=jnp.float32) * s, 'bfc': jnp.zeros((N_EXPERTS, HIDDEN), dtype=jnp.float32), 'Wproj': jax.random.normal(ks[5], (N_EXPERTS, HIDDEN, N_EMBD), dtype=jnp.float32) * s, 'bproj': jnp.zeros((N_EXPERTS, N_EMBD), dtype=jnp.float32)}
    _L3_ffn_in = _L3_ffn_setup()
    _L3_c = _w((lambda *s: np.random.randn(*s).astype(np.float32) * 0.05)(16, 128))
    _L3_wmod = _w((lambda *s: np.random.randn(*s).astype(np.float32) * 0.05)(128, 6 * 128) * 128 ** (-0.5))
    _d = {'L0_attn_x': _L0_attn_in['x'], 'L0_attn_Wq': _L0_attn_in['Wq'], 'L0_attn_bq': _L0_attn_in['bq'], 'L0_attn_Wk': _L0_attn_in['Wk'], 'L0_attn_bk': _L0_attn_in['bk'], 'L0_attn_Wv': _L0_attn_in['Wv'], 'L0_attn_bv': _L0_attn_in['bv'], 'L0_attn_Wo': _L0_attn_in['Wo'], 'L0_attn_bo': _L0_attn_in['bo'], 'L0_ffn_alpha': _L0_ffn_in['alpha'], 'L0_ffn_w_gate': _L0_ffn_in['w_gate'], 'L0_ffn_b_gate': _L0_ffn_in['b_gate'], 'L0_ffn_W1m': _L0_ffn_in['W1m'], 'L0_ffn_b1m': _L0_ffn_in['b1m'], 'L0_ffn_W2m': _L0_ffn_in['W2m'], 'L0_ffn_b2m': _L0_ffn_in['b2m'], 'L0_ffn_W1e': _L0_ffn_in['W1e'], 'L0_ffn_b1e': _L0_ffn_in['b1e'], 'L0_ffn_W2e': _L0_ffn_in['W2e'], 'L0_ffn_b2e': _L0_ffn_in['b2e'], 'L0_c': _L0_c, 'L0_wmod': _L0_wmod, 'L1_attn_W_qkv': _L1_attn_in['W_qkv'], 'L1_attn_W_out': _L1_attn_in['W_out'], 'L1_ffn_wqkv': _L1_ffn_in['wqkv'], 'L1_ffn_q_scale': _L1_ffn_in['q_scale'], 'L1_ffn_k_scale': _L1_ffn_in['k_scale'], 'L1_ffn_wo': _L1_ffn_in['wo'], 'L1_ffn_ln_g': _L1_ffn_in['ln_g'], 'L1_ffn_ln_b': _L1_ffn_in['ln_b'], 'L1_ffn_w1': _L1_ffn_in['w1'], 'L1_ffn_b1': _L1_ffn_in['b1'], 'L1_ffn_w2': _L1_ffn_in['w2'], 'L1_ffn_b2': _L1_ffn_in['b2'], 'L1_c': _L1_c, 'L1_wmod': _L1_wmod, 'L2_attn_Wq': _L2_attn_in['Wq'], 'L2_attn_Wk': _L2_attn_in['Wk'], 'L2_attn_Wv': _L2_attn_in['Wv'], 'L2_attn_Wo': _L2_attn_in['Wo'], 'L2_ffn_wg': _L2_ffn_in['wg'], 'L2_ffn_we': _L2_ffn_in['we'], 'L2_c': _L2_c, 'L2_wmod': _L2_wmod, 'L3_attn_wq': _L3_attn_in['wq'], 'L3_attn_bq': _L3_attn_in['bq'], 'L3_attn_wk': _L3_attn_in['wk'], 'L3_attn_bk': _L3_attn_in['bk'], 'L3_attn_wv': _L3_attn_in['wv'], 'L3_attn_bv': _L3_attn_in['bv'], 'L3_attn_wo': _L3_attn_in['wo'], 'L3_attn_bo': _L3_attn_in['bo'], 'L3_ffn_Wfc_s': _L3_ffn_in['Wfc_s'], 'L3_ffn_bfc_s': _L3_ffn_in['bfc_s'], 'L3_ffn_Wproj_s': _L3_ffn_in['Wproj_s'], 'L3_ffn_bproj_s': _L3_ffn_in['bproj_s'], 'L3_ffn_Wr': _L3_ffn_in['Wr'], 'L3_ffn_Wfc': _L3_ffn_in['Wfc'], 'L3_ffn_bfc': _L3_ffn_in['bfc'], 'L3_ffn_Wproj': _L3_ffn_in['Wproj'], 'L3_ffn_bproj': _L3_ffn_in['bproj'], 'L3_c': _L3_c, 'L3_wmod': _L3_wmod}
    _x0 = _d['L0_attn_x']
    _d['L0_attn_x'] = jax.random.normal(jax.random.fold_in(jax.random.key(seed), 1), (16, 512, 128), dtype=_x0.dtype)
    del _x0
    return _d

def reference(L0_attn_x, L0_attn_Wq, L0_attn_bq, L0_attn_Wk, L0_attn_bk, L0_attn_Wv, L0_attn_bv, L0_attn_Wo, L0_attn_bo, L0_ffn_alpha, L0_ffn_w_gate, L0_ffn_b_gate, L0_ffn_W1m, L0_ffn_b1m, L0_ffn_W2m, L0_ffn_b2m, L0_ffn_W1e, L0_ffn_b1e, L0_ffn_W2e, L0_ffn_b2e, L0_c, L0_wmod, L1_attn_W_qkv, L1_attn_W_out, L1_ffn_wqkv, L1_ffn_q_scale, L1_ffn_k_scale, L1_ffn_wo, L1_ffn_ln_g, L1_ffn_ln_b, L1_ffn_w1, L1_ffn_b1, L1_ffn_w2, L1_ffn_b2, L1_c, L1_wmod, L2_attn_Wq, L2_attn_Wk, L2_attn_Wv, L2_attn_Wo, L2_ffn_wg, L2_ffn_we, L2_c, L2_wmod, L3_attn_wq, L3_attn_bq, L3_attn_wk, L3_attn_bk, L3_attn_wv, L3_attn_bv, L3_attn_wo, L3_attn_bo, L3_ffn_Wfc_s, L3_ffn_bfc_s, L3_ffn_Wproj_s, L3_ffn_bproj_s, L3_ffn_Wr, L3_ffn_Wfc, L3_ffn_bfc, L3_ffn_Wproj, L3_ffn_bproj, L3_c, L3_wmod):

    def _L0_attn_ref(x, Wq, bq, Wk, bk, Wv, bv, Wo, bo):
        import jax, jax.numpy as jnp
        import numpy as np
        EMB_DIM = 128
        N_HEADS = 16
        HEAD_DIM = EMB_DIM // N_HEADS
        SEQ = 256
        BSZ = 2

        def _rope_pair(q, k):
            bsz, seq_len, d_model = q.shape
            freq_range = jnp.arange(d_model // 2, dtype=jnp.float32)
            freq_cis = jnp.power(10000.0, -2.0 * freq_range / d_model)
            pos = jnp.arange(seq_len, dtype=jnp.float32)
            freq = jnp.einsum('i,j->ij', pos, freq_cis)
            sin_e = jnp.sin(freq)[None]
            cos_e = jnp.cos(freq)[None]
            q_even, q_odd = (q[..., ::2], q[..., 1::2])
            k_even, k_odd = (k[..., ::2], k[..., 1::2])
            q_rot = jnp.concatenate([q_even * cos_e - q_odd * sin_e, q_even * sin_e - q_odd * cos_e], axis=-1)
            k_rot = jnp.concatenate([k_even * cos_e - k_odd * sin_e, k_even * sin_e - k_odd * cos_e], axis=-1)
            return (q_rot, k_rot)
        bsz, n, d = x.shape
        Q = x @ Wq + bq
        K = x @ Wk + bk
        V = x @ Wv + bv
        Q, K = _rope_pair(Q, K)
        Q = Q.reshape(bsz, n, N_HEADS, HEAD_DIM).transpose(0, 2, 1, 3)
        K = K.reshape(bsz, n, N_HEADS, HEAD_DIM).transpose(0, 2, 1, 3)
        V = V.reshape(bsz, n, N_HEADS, HEAD_DIM).transpose(0, 2, 1, 3)
        scores = jnp.einsum('bhqd,bhkd->bhqk', Q, K)
        causal = jnp.triu(jnp.ones((n, n), dtype=bool), k=1)
        scores = jnp.where(causal, -jnp.inf, scores)
        attn = jax.nn.softmax(scores / jnp.sqrt(jnp.float32(HEAD_DIM)), axis=-1)
        ctx = jnp.einsum('bhqk,bhkd->bhqd', attn, V)
        ctx = ctx.transpose(0, 2, 1, 3).reshape(bsz, n, d)
        return ctx @ Wo + bo

    def _L0_ffn_ref(x, alpha, w_gate, b_gate, W1m, b1m, W2m, b2m, W1e, b1e, W2e, b2e):
        import jax, jax.numpy as jnp
        import numpy as np
        from jax import lax
        B, N, D, H, E, K = (16, 128, 128, 512, 8, 2)
        main = jax.nn.gelu(x @ W1m + b1m) @ W2m + b2m
        logits = jnp.mean(x, axis=1) @ w_gate + b_gate
        probs = jax.nn.softmax(logits, axis=-1)
        top_vals, top_idx = lax.top_k(probs, K)
        gate_w = top_vals / jnp.sum(top_vals, axis=-1, keepdims=True)
        W1g = W1e[top_idx]
        b1g = b1e[top_idx]
        W2g = W2e[top_idx]
        b2g = b2e[top_idx]
        h = jax.nn.gelu(jnp.einsum('bnd,bkdh->bknh', x, W1g) + b1g[:, :, None, :])
        eo = jnp.einsum('bknh,bkhd->bknd', h, W2g) + b2g[:, :, None, :]
        expert_out = jnp.einsum('bk,bknd->bnd', gate_w, eo)
        a = jnp.clip(alpha, 0.1, 1.0)
        return a * main + (1.0 - a) * expert_out

    def _L1_attn_ref(x, W_qkv, W_out):
        import jax, jax.numpy as jnp
        import numpy as np
        B, S, D = x.shape
        head_dim = W_qkv.shape[-1] // 3
        qkv = jnp.einsum('bsd,ndh->bnsh', x, W_qkv)
        q, k, v = jnp.split(qkv, 3, axis=-1)
        scale = jnp.asarray(1.0 / np.sqrt(head_dim), dtype=x.dtype)
        attn = jnp.einsum('bnqh,bnkh->bnqk', q, k) * scale
        mask = jnp.asarray(-10000000000.0, dtype=x.dtype) * (1.0 - jnp.tril(jnp.ones((S, S), dtype=x.dtype)))
        attn = jax.nn.softmax(attn + mask, axis=-1)
        out = jnp.einsum('bnqk,bnkh->bnqh', attn, v)
        out = out.reshape(B, -1, S)
        return jnp.einsum('bds,nhd->bsd', out, W_out)

    def _L1_ffn_ref(x, wqkv, q_scale, k_scale, wo, ln_g, ln_b, w1, b1, w2, b2):
        import jax, jax.numpy as jnp
        import numpy as np
        DIM = 128
        DEPTH = 2
        HEADS = 8
        DIM_HEAD = 64
        WINDOW = 64
        INNER = HEADS * DIM_HEAD
        HID = int(DIM * 4 * 2 / 3)
        B, N = (2, 1024)
        QK_SCALE = 8.0

        def shift_token(t):
            t1, t2 = jnp.split(t, 2, axis=-1)
            t2 = jnp.pad(t2, ((0, 0), (1, 0), (0, 0)))[:, :-1]
            return jnp.concatenate([t1, t2], axis=-1)

        def l2norm(t):
            return t / jnp.clip(jnp.linalg.norm(t, axis=-1, keepdims=True), 1e-12)

        def rotate_half(x):
            x1, x2 = jnp.split(x, 2, axis=-1)
            return jnp.concatenate([-x2, x1], axis=-1)

        def rotary_xpos(q, k):
            n = q.shape[-2]
            half_idx = jnp.arange(0, DIM_HEAD, 2, dtype=jnp.float32)
            inv_freq = 1.0 / 10000.0 ** (half_idx / DIM_HEAD)
            t = jnp.arange(n, dtype=jnp.float32)
            freqs = t[:, None] * inv_freq[None, :]
            freqs = jnp.concatenate([freqs, freqs], axis=-1)
            base = (half_idx + 0.4 * DIM_HEAD) / (1.4 * DIM_HEAD)
            power = (t - n // 2) / float(WINDOW // 2)
            scale = base[None, :] ** power[:, None]
            scale = jnp.concatenate([scale, scale], axis=-1)
            cos, sin = (jnp.cos(freqs), jnp.sin(freqs))
            q = q * cos * scale + rotate_half(q) * sin * scale
            k = k * cos / scale + rotate_half(k) * sin / scale
            return (q, k)

        def local_attention(q, k, v):
            b, h, n, d = q.shape
            w = n // WINDOW
            bq = q.reshape(b, h, w, WINDOW, d) * QK_SCALE
            bk = k.reshape(b, h, w, WINDOW, d)
            bv = v.reshape(b, h, w, WINDOW, d)

            def look_around(t):
                p = jnp.pad(t, ((0, 0), (0, 0), (1, 0), (0, 0), (0, 0)))
                return jnp.concatenate([p[:, :, :w], p[:, :, 1:]], axis=3)
            bk, bv = (look_around(bk), look_around(bv))
            bt = jnp.arange(n).reshape(w, WINDOW)
            btp = jnp.pad(bt, ((1, 0), (0, 0)), constant_values=-1)
            btk = jnp.concatenate([btp[:w], btp[1:]], axis=1)
            sim = jnp.einsum('bhwid,bhwjd->bhwij', bq, bk)
            i = bt[:, :, None]
            j = btk[:, None, :]
            mask = (i < j) | (i > j + WINDOW) | (j == -1)
            sim = jnp.where(mask, -jnp.finfo(sim.dtype).max, sim)
            attn = jax.nn.softmax(sim, axis=-1)
            out = jnp.einsum('bhwij,bhwjd->bhwid', attn, bv)
            return out.reshape(b, h, n, d)

        def _layer(x, wqkv, qs, ksc, wo, lg, lb, w1, b1, w2, b2):
            b, n, _ = x.shape
            h = shift_token(x)
            qkv = h @ wqkv
            q, k, v = jnp.split(qkv, 3, axis=-1)
            to_heads = lambda t: t.reshape(b, n, HEADS, DIM_HEAD).transpose(0, 2, 1, 3)
            q, k, v = (to_heads(q), to_heads(k), to_heads(v))
            q = l2norm(q) * qs
            k = l2norm(k) * ksc
            q, k = rotary_xpos(q, k)
            o = local_attention(q, k, v)
            o = o.transpose(0, 2, 1, 3).reshape(b, n, INNER)
            x = x + o @ wo
            h = shift_token(x)
            mu = h.mean(-1, keepdims=True)
            var = h.var(-1, keepdims=True)
            h = (h - mu) / jnp.sqrt(var + 1e-05) * lg + lb
            h = h @ w1 + b1
            a, g = jnp.split(h, 2, axis=-1)
            h = a * jax.nn.gelu(g, approximate=False)
            x = x + h @ w2 + b2
            return x
        for l in range(DEPTH):
            x = _layer(x, wqkv[l], q_scale[l], k_scale[l], wo[l], ln_g[l], ln_b[l], w1[l], b1[l], w2[l], b2[l])
        return x

    def _L2_attn_ref(x, Wq, Wk, Wv, Wo):
        import jax, jax.numpy as jnp
        import numpy as np
        SEQ_LEN = 256
        DIM_EMB = 128
        DIM_K = 128
        DIM_V = 128
        q = jnp.einsum('bse,ek->bsk', x, Wq)
        k = jnp.einsum('bse,ek->bsk', x, Wk)
        v = jnp.einsum('bse,ev->bsv', x, Wv)
        scores = jnp.einsum('bqk,bsk->bqs', q, k)
        S = x.shape[1]
        causal_mask = jnp.triu(jnp.ones((S, S), dtype=bool), k=1)
        m_inf = -jnp.finfo(scores.dtype).max
        scores = jnp.where(causal_mask[None, :, :], m_inf, scores)
        attn = jax.nn.softmax(scores * DIM_K ** (-0.5), axis=-1)
        out = jnp.einsum('bqs,bsv->bqv', attn, v)
        return jnp.einsum('bqv,vo->bqo', out, Wo)

    def _L2_ffn_ref(x, wg, we):
        import jax, jax.numpy as jnp
        import numpy as np
        E = 128
        D = 128
        C = 32
        B, S, d = x.shape
        xt = x.reshape(-1, d)
        T = xt.shape[0]
        logits = xt @ wg
        gates = jax.nn.softmax(logits, axis=-1)
        e1 = jnp.argmax(gates, axis=-1)
        mask1 = jax.nn.one_hot(e1, E, dtype=logits.dtype)
        logits2 = jnp.where(mask1 > 0, -jnp.inf, logits)
        e2 = jnp.argmax(logits2, axis=-1)
        mask2 = jax.nn.one_hot(e2, E, dtype=logits.dtype)
        g1 = jnp.take_along_axis(gates, e1[:, None], 1)[:, 0]
        g2 = jnp.take_along_axis(gates, e2[:, None], 1)[:, 0]
        denom = jnp.maximum(g1 + g2, jnp.finfo(gates.dtype).eps)
        g1, g2 = (g1 / denom, g2 / denom)
        loc1 = jnp.take_along_axis(jnp.cumsum(mask1, axis=0), e1[:, None], 1)[:, 0].astype(jnp.int32) - 1
        counts1 = mask1.sum(axis=0)
        loc2 = (jnp.take_along_axis(jnp.cumsum(mask2, axis=0), e2[:, None], 1)[:, 0] + counts1[e2]).astype(jnp.int32) - 1
        v1 = (loc1 < C).astype(xt.dtype)
        v2 = (loc2 < C).astype(xt.dtype)
        idx1 = e1.astype(jnp.int32) * C + jnp.minimum(loc1, C - 1)
        idx2 = e2.astype(jnp.int32) * C + jnp.minimum(loc2, C - 1)
        buf = jnp.zeros((E * C, d), dtype=xt.dtype)
        buf = buf.at[idx1].add(xt * v1[:, None])
        buf = buf.at[idx2].add(xt * v2[:, None])
        yb = jnp.einsum('ecd,edf->ecf', buf.reshape(E, C, d), we).reshape(E * C, d)
        y = (g1 * v1)[:, None] * yb[idx1] + (g2 * v2)[:, None] * yb[idx2]
        return y.reshape(B, S, d)

    def _L3_attn_ref(x, wq, bq, wk, bk, wv, bv, wo, bo):
        import jax, jax.numpy as jnp
        import numpy as np
        H = 16
        ROPE_BASE = 10000.0

        def _rotate_half(x):
            d = x.shape[-1]
            return jnp.concatenate((-x[..., d // 2:], x[..., :d // 2]), axis=-1)
        B, S, E = x.shape
        D = E // H

        def proj(w, b):
            return (x @ w.T + b).reshape(B, S, H, D).transpose(0, 2, 1, 3)
        q = proj(wq, bq)
        k = proj(wk, bk)
        v = proj(wv, bv)
        inv_freq = 1.0 / ROPE_BASE ** (jnp.arange(0, D, 2, dtype=jnp.float32) / D)
        freqs = jnp.arange(S, dtype=jnp.float32)[:, None] * inv_freq[None, :]
        cos = jnp.repeat(jnp.cos(freqs), 2, axis=-1)[None, None]
        sin = jnp.repeat(jnp.sin(freqs), 2, axis=-1)[None, None]
        q = q * cos + _rotate_half(q) * sin
        k = k * cos + _rotate_half(k) * sin
        scale = D ** (-0.5)
        scores = jnp.einsum('bhqd,bhkd->bhqk', q, k) * scale
        attn = jax.nn.softmax(scores, axis=-1)
        out = jnp.einsum('bhqk,bhkd->bhqd', attn, v)
        out = out.transpose(0, 2, 1, 3).reshape(B, S, E)
        return out @ wo.T + bo

    def _L3_ffn_ref(x, Wfc_s, bfc_s, Wproj_s, bproj_s, Wr, Wfc, bfc, Wproj, bproj):
        import jax, jax.numpy as jnp
        import numpy as np
        import math
        N_EMBD = 128
        HIDDEN = 4 * N_EMBD
        N_EXPERTS = 8
        TOP_K = 2
        B, T = (4, 256)

        def new_gelu(x):
            c = math.sqrt(2.0 / math.pi)
            return 0.5 * x * (1.0 + jnp.tanh(c * (x + 0.044715 * x * x * x)))

        def _moe_forward(x, Wfc_s, bfc_s, Wproj_s, bproj_s, Wr, Wfc, bfc, Wproj, bproj):
            Bb, Tt, C = x.shape
            xf = x.reshape(Bb * Tt, C)
            N = Bb * Tt
            shared = new_gelu(xf @ Wfc_s + bfc_s) @ Wproj_s + bproj_s
            logits = xf @ Wr
            probs = jax.nn.softmax(logits, axis=-1)
            topk_p, topk_i = jax.lax.top_k(probs, TOP_K)
            topk_p = topk_p / jnp.sum(topk_p, axis=-1, keepdims=True)
            gate = jnp.zeros((N, N_EXPERTS), dtype=xf.dtype)
            gate = gate.at[jnp.arange(N)[:, None], topk_i].add(topk_p)
            routed = jnp.zeros_like(xf)
            for e in range(N_EXPERTS):
                h = new_gelu(xf @ Wfc[e] + bfc[e]) @ Wproj[e] + bproj[e]
                routed = routed + h * gate[:, e:e + 1]
            return (shared + routed).reshape(Bb, Tt, C)
        return _moe_forward(x, Wfc_s, bfc_s, Wproj_s, bproj_s, Wr, Wfc, bfc, Wproj, bproj)
    x = L0_attn_x
    mod = (_silu(L0_c) @ L0_wmod).reshape(L0_c.shape[0], 6, 1, -1)
    sa, ca, ga, sb, cb, gb = (mod[:, 0], mod[:, 1], mod[:, 2], mod[:, 3], mod[:, 4], mod[:, 5])
    ga = (2 * (ga >= 0) - 1) * jnp.maximum(jnp.abs(ga), 0.25)
    gb = (2 * (gb >= 0) - 1) * jnp.maximum(jnp.abs(gb), 0.25)
    h = _layernorm(x, axis=-1) * (1 + ca) + sa
    x = x + ga * _L0_attn_ref(h, L0_attn_Wq, L0_attn_bq, L0_attn_Wk, L0_attn_bk, L0_attn_Wv, L0_attn_bv, L0_attn_Wo, L0_attn_bo)
    h = _layernorm(x, axis=-1) * (1 + cb) + sb
    x = x + gb * _L0_ffn_ref(h, L0_ffn_alpha, L0_ffn_w_gate, L0_ffn_b_gate, L0_ffn_W1m, L0_ffn_b1m, L0_ffn_W2m, L0_ffn_b2m, L0_ffn_W1e, L0_ffn_b1e, L0_ffn_W2e, L0_ffn_b2e)
    mod = (_silu(L1_c) @ L1_wmod).reshape(L1_c.shape[0], 6, 1, -1)
    sa, ca, ga, sb, cb, gb = (mod[:, 0], mod[:, 1], mod[:, 2], mod[:, 3], mod[:, 4], mod[:, 5])
    ga = (2 * (ga >= 0) - 1) * jnp.maximum(jnp.abs(ga), 0.25)
    gb = (2 * (gb >= 0) - 1) * jnp.maximum(jnp.abs(gb), 0.25)
    h = _layernorm(x, axis=-1) * (1 + ca) + sa
    x = x + ga * _L1_attn_ref(h, L1_attn_W_qkv, L1_attn_W_out)
    h = _layernorm(x, axis=-1) * (1 + cb) + sb
    x = x + gb * _L1_ffn_ref(h, L1_ffn_wqkv, L1_ffn_q_scale, L1_ffn_k_scale, L1_ffn_wo, L1_ffn_ln_g, L1_ffn_ln_b, L1_ffn_w1, L1_ffn_b1, L1_ffn_w2, L1_ffn_b2)
    mod = (_silu(L2_c) @ L2_wmod).reshape(L2_c.shape[0], 6, 1, -1)
    sa, ca, ga, sb, cb, gb = (mod[:, 0], mod[:, 1], mod[:, 2], mod[:, 3], mod[:, 4], mod[:, 5])
    ga = (2 * (ga >= 0) - 1) * jnp.maximum(jnp.abs(ga), 0.25)
    gb = (2 * (gb >= 0) - 1) * jnp.maximum(jnp.abs(gb), 0.25)
    h = _layernorm(x, axis=-1) * (1 + ca) + sa
    x = x + ga * _L2_attn_ref(h, L2_attn_Wq, L2_attn_Wk, L2_attn_Wv, L2_attn_Wo)
    h = _layernorm(x, axis=-1) * (1 + cb) + sb
    x = x + gb * _L2_ffn_ref(h, L2_ffn_wg, L2_ffn_we)
    mod = (_silu(L3_c) @ L3_wmod).reshape(L3_c.shape[0], 6, 1, -1)
    sa, ca, ga, sb, cb, gb = (mod[:, 0], mod[:, 1], mod[:, 2], mod[:, 3], mod[:, 4], mod[:, 5])
    ga = (2 * (ga >= 0) - 1) * jnp.maximum(jnp.abs(ga), 0.25)
    gb = (2 * (gb >= 0) - 1) * jnp.maximum(jnp.abs(gb), 0.25)
    h = _layernorm(x, axis=-1) * (1 + ca) + sa
    x = x + ga * _L3_attn_ref(h, L3_attn_wq, L3_attn_bq, L3_attn_wk, L3_attn_bk, L3_attn_wv, L3_attn_bv, L3_attn_wo, L3_attn_bo)
    h = _layernorm(x, axis=-1) * (1 + cb) + sb
    x = x + gb * _L3_ffn_ref(h, L3_ffn_Wfc_s, L3_ffn_bfc_s, L3_ffn_Wproj_s, L3_ffn_bproj_s, L3_ffn_Wr, L3_ffn_Wfc, L3_ffn_bfc, L3_ffn_Wproj, L3_ffn_bproj)
    return x

_drawn_inputs = setup_inputs


def setup_inputs(seed=0):
    import zlib

    import numpy as np

    out = dict(_drawn_inputs(seed))
    spreads = {'L0_ffn_b_gate': (0.0, 0.8),
     'L0_ffn_b1m': (0.0, 0.8),
     'L0_ffn_b2m': (0.0, 0.297),
     'L0_ffn_b1e': (0.0, 0.8),
     'L0_ffn_b2e': (0.0, 0.8),
     'L1_ffn_q_scale': (1.0, 0.6),
     'L1_ffn_k_scale': (1.0, 0.6),
     'L1_ffn_ln_g': (1.0, 0.6),
     'L1_ffn_ln_b': (0.0, 0.8),
     'L1_ffn_b1': (0.0, 0.8),
     'L1_ffn_b2': (0.0, 0.8),
     'L3_ffn_bfc_s': (0.0, 2.0),
     'L3_ffn_bproj_s': (0.0, 2.0),
     'L3_ffn_bfc': (0.0, 2.0),
     'L3_ffn_bproj': (0.0, 2.0)}
    factors = {'L0_attn_bq': 23.619,
     'L0_attn_bk': 55.964,
     'L0_attn_bv': 8.0,
     'L0_attn_bo': 8.0,
     'L0_ffn_w_gate': 8.0,
     'L0_ffn_W1m': 4.433,
     'L0_ffn_W2m': 4.07,
     'L0_ffn_W1e': 8.0,
     'L0_ffn_W2e': 8.0,
     'L1_ffn_wqkv': 6.686,
     'L1_ffn_wo': 6.785,
     'L1_ffn_w1': 8.0,
     'L1_ffn_w2': 8.0,
     'L2_ffn_wg': 22.672,
     'L2_ffn_we': 22.632,
     'L3_attn_wq': 33.081,
     'L3_attn_bq': 200.0,
     'L3_attn_wk': 31.681,
     'L3_attn_bk': 200.0,
     'L3_attn_wv': 8.0,
     'L3_attn_bv': 64.0,
     'L3_attn_wo': 8.0,
     'L3_attn_bo': 200.0,
     'L3_ffn_Wfc_s': 15.827,
     'L3_ffn_Wproj_s': 10.9,
     'L3_ffn_Wr': 3.403,
     'L3_ffn_Wfc': 6.232,
     'L3_ffn_Wproj': 5.629,
     'L2_attn_Wq': 8.0,
     'L2_attn_Wk': 8.0,
     'L2_attn_Wv': 4.924,
     'L2_attn_Wo': 4.988,
     'L2_c': 4.653,
     'L2_wmod': 4.703}
    for name, (base, spread) in spreads.items():
        noise = np.random.default_rng([zlib.crc32(name.encode()), seed]).standard_normal(out[name].shape)
        drawn = base * np.exp(spread * noise) if base else spread * noise
        out[name] = jnp.asarray(drawn.astype(out[name].dtype))
    for name, factor in factors.items():
        out[name] = (out[name] * factor).astype(out[name].dtype)
    return out
```

```python
from contextlib import ExitStack

import concourse.bass as bass
import numpy as np
from concourse import mybir

F32 = mybir.dt.float32
BF16 = mybir.dt.bfloat16
U32 = mybir.dt.uint32
I32 = mybir.dt.int32
ALU = mybir.AluOpType
ACT = mybir.ActivationFunctionType
AX = mybir.AxisListType.X

P = 128
B = 16
S = 512
NT = S // P
H16, DH8 = 16, 8
BIG = -1e30


class Signal:

    def __init__(self, ctx, nc, name, per, credit=0):
        self.sem = nc.alloc_semaphore(name)
        self.per, self.credit = per, credit

    def wait(self, eng, step, k):
        value = step * self.per + (k + self.credit)
        if isinstance(value, int) and value <= self.credit:
            return
        eng.wait_ge(self.sem, value)


class Chain:

    def __init__(self, ctx, nc, name, per):
        self.sem = nc.alloc_semaphore(name)
        self.per, self.k = per, 0

    def start(self, step):
        assert self.k in (0, self.per), (self.k, self.per)
        self.step, self.k = step, 0

    def link(self, eng, ins):
        self.k += 1
        ins.then_inc(self.sem, 1)
        eng.wait_ge(self.sem, self.step * self.per + self.k)


def stand_alone(net, eng):
    eng.sem_inc(net.passed, 1)


class Net:
    pass


def load_shared(net, ctx):
    nc, d = net.nc, net.d

    def sb(name, shape, dt=F32):
        return ctx.enter_context(nc.sbuf_tensor(name, shape, dt))

    net.passed = nc.alloc_semaphore("passed")
    net.X = sb("X", [P, B, S])
    net.MOD = sb("MOD", [P, 4, 6, B])
    net.ident = sb("ident", [P, P])
    net.center = sb("center", [P, P])
    net.mean = sb("mean", [P, P])
    net.ident_b = sb("ident_b", [P, P], BF16)
    net.H = sb("H", [P, B, S])
    net.eps = sb("eps", [P, 1])
    net.w3 = sb("w3", [P, B * 3])
    net.chosen = sb("chosen", [1, B * 2], U32)
    net.slot = sb("slot", [P, 2, B * NT], U32)
    net.wgt = sb("wgt", [P, 2, B * NT])
    net.mask_qk = sb("mask_qk", [P, P], BF16)
    net.mask_kq = sb("mask_kq", [P, P], BF16)


def modulation_phase(net):
    nc, d = net.nc, net.d
    with ExitStack() as ctx:
        def sb(name, shape, dt=F32):
            return ctx.enter_context(nc.sbuf_tensor(name, shape, dt))

        cT = sb("cT", [P, 4, B])
        sig = sb("sig", [P, 4, B])
        wm = sb("wm", [P, 4, 6 * P])
        maskf = sb("maskf", [P, 2, P])
        ge = sb("ge", [P, 4, B])
        ab = sb("ab", [P, 4, B])
        ps = ctx.enter_context(nc.psum_tensor("mod_ps", [P, 4, 6, B], F32))
        loaded = nc.alloc_semaphore("mod_loaded")
        x_loaded = nc.alloc_semaphore("x_loaded")
        ex = nc.alloc_semaphore("mod_exp")
        si = nc.alloc_semaphore("mod_silu")
        mm = nc.alloc_semaphore("mod_products")
        ch = nc.alloc_semaphore("mod_dve_chain")
        block = ctx.enter_context(nc.Block())

        @block.sync
        def _(sp):
            sp.dma_start(cT[:], d["cT"].rearrange("l p b -> p l b")).then_inc(loaded, 16)
            sp.dma_start(wm[:], d["wmod"].rearrange("l p n -> p l n")).then_inc(loaded, 16)
            sp.dma_start(net.ident[:], d["k_ident"]).then_inc(loaded, 16)
            sp.dma_start(net.center[:], d["k_center"]).then_inc(loaded, 16)
            sp.dma_start(net.mean[:], d["k_mean"]).then_inc(loaded, 16)
            sp.dma_start(maskf[:], d["k_mask"].rearrange("a p n -> p a n")).then_inc(loaded, 16)
            for b in range(0, B, 4):
                sp.dma_start(net.X[:, b:b + 4], d["xT"][:, b:b + 4]).then_inc(x_loaded, 16)
            sp.wait_ge(x_loaded, 64)

        @block.scalar
        def _(act):
            act.wait_ge(loaded, 96)
            nc.scalar.activation(sig[:], cT[:], ACT.Exp, scale=-1.0).then_inc(ex, 1)

        @block.vector
        def _(dve):
            n = [0]

            def link(ins):
                n[0] += 1
                ins.then_inc(ch, 1)
                dve.wait_ge(ch, n[0])

            dve.wait_ge(ex, 1)
            link(nc.vector.tensor_scalar(sig[:], sig[:], 1.0, None, ALU.add))
            link(nc.vector.reciprocal(sig[:], sig[:]))
            nc.vector.tensor_tensor(sig[:], sig[:], cT[:], ALU.mult).then_inc(si, 1)
            nc.vector.memset(net.eps[:], 1e-5)
            nc.vector.tensor_copy(net.ident_b[:], net.ident[:])
            nc.vector.tensor_copy(net.mask_qk[:], maskf[:, 0])
            nc.vector.tensor_copy(net.mask_kq[:], maskf[:, 1])
            dve.wait_ge(mm, 1)
            M = net.MOD
            link(nc.vector.tensor_copy(M[:], ps[:]))
            for j in (1, 4):
                link(nc.vector.tensor_scalar(M[:, :, j], M[:, :, j], 1.0, None, ALU.add))
            for j in (2, 5):
                link(nc.vector.tensor_scalar(ge[:], M[:, :, j], 0.0, None, ALU.is_ge))
                link(nc.vector.tensor_scalar(ge[:], ge[:], 2.0, -1.0, ALU.mult, ALU.add))
                link(nc.vector.tensor_tensor(ab[:], M[:, :, j], ge[:], ALU.mult))
                link(nc.vector.tensor_scalar(ab[:], ab[:], 0.25, None, ALU.max))
                link(nc.vector.tensor_tensor(M[:, :, j], ge[:], ab[:], ALU.mult))

        @block.tensor
        def _(pe):
            pe.wait_ge(si, 1)
            for l in range(4):
                for j in range(6):
                    last = nc.tensor.matmul(ps[:, l, j], wm[:, l, j * P:(j + 1) * P], sig[:, l],
                                            start=True, stop=True)
            last.then_inc(mm, 1)


def norm_phase(net, name, layer, part, small=None):
    nc, X, H = net.nc, net.X, net.H
    if small is not None:
        X, H = net.H, net.N
    shift, scale = net.MOD[:, layer, 3 * part], net.MOD[:, layer, 3 * part + 1]
    with ExitStack() as ctx:
        def sb(n, shape, dt=F32):
            return ctx.enter_context(nc.sbuf_tensor(name + n, shape, dt))

        sq = sb("sq", [P, 2, S])
        xs = sb("xs", [P, 4, S])
        dev = sb("dev", [P, 2, NT])
        diag = sb("diag", [P, 2, NT, P])
        ones = sb("ones", [P, P])
        h0 = sb("h0", [P, 2, S])
        xc = ctx.enter_context(nc.psum_tensor(name + "xc", [P, 4, S], F32))
        var = ctx.enter_context(nc.psum_tensor(name + "var", [P, 2, S], F32))
        rstd = ctx.enter_context(nc.psum_tensor(name + "rstd", [P, 2, S], F32))
        sig = lambda n, per: Signal(ctx, nc, name + n, per)
        filled = nc.alloc_semaphore(name + "filled")
        centered = sig("centered", 1)
        copied = sig("copied", 1)
        squared = sig("squared", 1)
        variance = sig("variance", 1)
        deviation = sig("deviation", 1)
        inverse = sig("inverse", 1)
        diagonal = sig("diagonal", 1)
        spread = sig("spread", 1)
        normed = sig("normed", 1)
        shifted = sig("shifted", 1)
        block = ctx.enter_context(nc.Block())

        def nothing(b, j):
            pass

        def steps(eng, first, second, third):
            for b in range(4):
                first(b, b)
                if b >= 1:
                    second(b - 1, b - 1)
                if b >= 2:
                    third(b - 2, b - 2)
            with eng.Fori(1, B // 4) as i:
                for j in range(4):
                    first(i * 4 + j, j)
                    second(i * 4 + (j - 1), (j + 3) % 4)
                    third(i * 4 + (j - 2), (j + 2) % 4)
            second(B - 1, 3)
            third(B - 2, 2)
            third(B - 1, 3)

        @block.tensor
        def _(pe):
            pe.wait_ge(filled, 1)

            def first(b, j):
                copied.wait(pe, b - 4, 1)
                squared.wait(pe, b - 4, 1)
                if small is None:
                    mm = nc.tensor.matmul(xc[:, j], net.center[:], X[:, b], start=True, stop=True)
                else:
                    nc.tensor.matmul(xc[:, j], net.split_center[:, 0], X[:, b], start=True, stop=False)
                    mm = nc.tensor.matmul(xc[:, j, 1:S], net.split_center[:, 1], X[:, b, 0:S - 1], start=False, stop=True)
                mm.then_inc(centered.sem, 1)

            def second(b, j):
                squared.wait(pe, b, 1)
                deviation.wait(pe, b - 2, 1)
                for t in range(NT):
                    mm = nc.tensor.matmul(var[:, j % 2, t:t + 1], sq[:, j % 2, t * P:(t + 1) * P], net.mean[:, 0:1],
                                          start=True, stop=True)
                mm.then_inc(variance.sem, 1)

            def third(b, j):
                diagonal.wait(pe, b, 1)
                normed.wait(pe, b - 2, 1)
                nc.tensor.matmul(rstd[:, j % 2], ones[:], diag[:, j % 2].rearrange("p t n -> p (t n)"),
                                 start=True, stop=True).then_inc(spread.sem, 1)
            steps(pe, first, second, third)

        @block.scalar
        def _(act):
            def first(b, j):
                centered.wait(act, b, 1)
                variance.wait(act, b - 2, 1)
                nc.scalar.activation(sq[:, j % 2], xc[:, j], ACT.Square).then_inc(squared.sem, 1)
                normed.wait(act, b - 4, 1)
                nc.scalar.activation(xs[:, j], xc[:, j], ACT.Copy).then_inc(copied.sem, 1)

            def second(b, j):
                variance.wait(act, b, 1)
                inverse.wait(act, b - 2, 1)
                diagonal.wait(act, b - 2, 1)
                nc.scalar.activation(dev[:, j % 2], var[:, j % 2, 0:NT], ACT.Sqrt, bias=net.eps[:, 0:1]).then_inc(deviation.sem, 1)

            def third(b, j):
                normed.wait(act, b, 1)
                g, s = (col(scale, b), col(shift, b)) if small is None else (net.ln[:, 0, small:small + 1], net.ln[:, 1, small:small + 1])
                nc.scalar.activation(H[:, b], h0[:, j % 2], ACT.Identity, bias=s, scale=g).then_inc(shifted.sem, 1)
            steps(act, first, second, third)

        @block.vector
        def _(dve):
            nc.vector.memset(ones[:], 1.0).then_inc(filled, 1)

            def second(b, j):
                deviation.wait(dve, b, 1)
                nc.vector.reciprocal(dev[:, j % 2], dev[:, j % 2]).then_inc(inverse.sem, 1)
                inverse.wait(dve, b, 1)
                spread.wait(dve, b - 2, 1)
                nc.vector.tensor_tensor(diag[:, j % 2], net.ident[:].unsqueeze(1).broadcast_to([P, NT, P]),
                                        dev[:, j % 2].unsqueeze(2).broadcast_to([P, NT, P]), ALU.mult).then_inc(diagonal.sem, 1)

            def third(b, j):
                spread.wait(dve, b, 1)
                copied.wait(dve, b, 1)
                shifted.wait(dve, b - 2, 1)
                nc.vector.tensor_tensor(h0[:, j % 2], xs[:, j], rstd[:, j % 2], ALU.mult).then_inc(normed.sem, 1)
            steps(dve, nothing, second, third)


def col(t, b):
    return t[:, bass.ds(b, 1)]


TERM_RUNS = [(0, 3, 0), (3, 2, 1), (5, 1, 2)]
MROW = 96
G = 4


def heads16_phase(net, name, layer, causal, rope, w_sum):
    nc, X, H, d = net.nc, net.X, net.H, net.d
    gate = net.MOD[:, layer, 2]
    scale = float(1.0 / np.sqrt(np.float32(DH8)))
    with ExitStack() as ctx:
        def sb(n, shape, dt=F32):
            return ctx.enter_context(nc.sbuf_tensor(name + n, shape, dt))

        def psum(n, shape):
            return ctx.enter_context(nc.psum_tensor(name + n, shape, F32))

        def sig(n, per):
            return Signal(ctx, nc, name + n, per)

        NQK = 4 if rope else 2
        RING = 6
        wqk = sb("wqk", [P, NQK, P])
        wv = sb("wv", [P, P])
        bqk = sb("bqk", [P, NQK])
        bv = sb("bv", [P, P])
        turn = sb("turn", [P, 2, S]) if rope else None
        wo = sb("wo", [P, G, P])
        bo = sb("bo", [P, 1])
        gbo = sb("gbo", [P, B])
        qk = sb("qk", [P, 2, S])
        t2 = sb("t2", [P, S])
        qkp = sb("qkp", [P, 2, 3, S], BF16)
        QS = sb("QS", [P, 2, H16, S], BF16)
        KS = sb("KS", [P, 2, H16, S], BF16)
        V = sb("V", [P, 2, NT, H16, 32])
        prob = sb("prob", [P, RING, S])
        neg = sb("neg", [P, NT, H16])
        mres = sb("mres", [H16, S])
        mparts = sb("mparts", [H16, 3, S], BF16)
        cn = sb("cn", [P, G, S])
        comp = sb("comp", [P, H16 * S // P])
        rs = sb("rs", [P, G, S])
        y = sb("y", [P, S])
        hcopy = sb("hcopy", [P, S])
        z = sb("z", [P, S]) if w_sum else None
        PA = psum("PA", [P, 2, S])
        PB = psum("PB", [P, 2, S])
        PO = psum("PO", [P, 2, S])
        PM = psum("PM", [P, 2, S])
        spill = nc.dram_tensor(name + "spill", [2, 2, 3, DH8, H16, S], BF16, kind="Internal").ap()
        inverses = nc.dram_tensor(name + "inverses", [4, G * S], F32, kind="Internal").ap()
        mixed = nc.dram_tensor(name + "mixed", [2, H16, 8, DH8, 64], F32, kind="Internal").ap() if w_sum else None

        loaded = nc.alloc_semaphore(name + "loaded")
        filled = nc.alloc_semaphore(name + "filled")
        wsum_done = nc.alloc_semaphore(name + "wsum_done")
        g_ready = nc.alloc_semaphore(name + "g_ready")
        projected = sig("projected", 2)
        v_made = sig("v_made", 1)
        turned = sig("turned", 2)
        v_ready = sig("v_ready", 1)
        parts = sig("parts", 2)
        spilled = sig("spilled", 6 * 16)
        stacked = [sig(f"stacked{g}", 6 * 16) for g in range(G)]
        a_done = sig("a_done", 64)
        maxed = sig("maxed", 64)
        m_turned = sig("m_turned", 1)
        m_parts = sig("m_parts", 1)
        m_rows = sig("m_rows", 48)
        b_done = sig("b_done", 64)
        exped = sig("exped", 64)
        pv_done = sig("pv_done", 64)
        c_raw = sig("c_raw", G)
        sums_in = sig("sums_in", 16)
        inverted = sig("inverted", 1)
        inv_out = sig("inv_out", 16)
        inv_in = sig("inv_in", 16 * 4)
        c_norm = sig("c_norm", 1)
        mixing = sig("mixing", 16 * H16)
        o_done = sig("o_done", 16 if w_sum else 1)
        y_done = sig("y_done", 1)
        x_done = Signal(ctx, nc, name + "x_done", 1, 1)
        h_here = sig("h_here", 1)
        turn_chain = Chain(ctx, nc, name + "turn_chain", 4 if rope else 0)
        m_chain = Chain(ctx, nc, name + "m_chain", 3)
        part_chain = Chain(ctx, nc, name + "part_chain", 6)
        LOADS = 7 if rope else (5 if not w_sum else 3)
        block = ctx.enter_context(nc.Block())

        def has(b):
            return not isinstance(b, int) or 0 <= b < B

        def steps(eng, step):
            for i in range(-1, 4):
                step(i, i % 2)
            with eng.Fori(2, B // 2 - 1) as pair:
                step(pair * 2, 0)
                step(pair * 2 + 1, 1)
            for i in range(B - 2, B + 2):
                step(i, i % 2)

        UNITS = [(g, t, j) for g in range(G) for t in range(NT) for j in range(G)]
        LEAD = 8
        LAG = 2
        Q_PROJ, K_PROJ, V_PROJ, O_PROJ = 8, 16, 26, 36

        @block.sync
        def _(sp):
            sp.dma_start(wqk[:], d[name + "wqk"].rearrange("j p n -> p j n")).then_inc(loaded, 16)
            sp.dma_start(wv[:], d[name + "wv"]).then_inc(loaded, 16)
            if w_sum:
                sp.dma_start(wo[:, 0], d[name + "wo"]).then_inc(loaded, 16)
            else:
                sp.dma_start(bqk[:], d[name + "bqk"]).then_inc(loaded, 16)
                sp.dma_start(bv[:], d[name + "bv"].partition_broadcast(P)).then_inc(loaded, 16)
                sp.dma_start(bo[:], d[name + "bo"]).then_inc(loaded, 16)
                sp.dma_start(turn[:], d[name + "turn"].rearrange("a p n -> p a n")).then_inc(loaded, 16)
                sp.dma_start(wo[:], d[name + "wo"].rearrange("g p n -> p g n")).then_inc(loaded, 16)
            sp.wait_ge(filled, 5)

            def step(i, par):
                if has(i - 2):
                    b, p = i - 2, par
                    inverted.wait(sp, b, 1)
                    sp.dma_start(inverses.rearrange("j (q n) -> (j q) n", q=P // 4), comp[:]).then_inc(inv_out.sem, 16)
                    inv_out.wait(sp, b, 16)
                    c_norm.wait(sp, b - 1, 1)
                    for j in range(4):
                        sp.dma_start(rs[32 * j:32 * j + DH8].rearrange("p g n -> p (g n)"),
                                     inverses[j].partition_broadcast(DH8)).then_inc(inv_in.sem, 16)
                if w_sum and has(i - 2):
                    c_norm.wait(sp, b, 1)
                    for g in range(G):
                        for j in range(G):
                            sp.dma_start(mixed[p, g * G + j].rearrange("s dd l -> dd s l"),
                                         cn[32 * j:32 * j + DH8, g].rearrange("dd (s l) -> dd s l", s=8)
                                         ).then_inc(mixing.sem, 16)
                    mixing.wait(sp, b, 16 * H16)
                    stand_alone(net, sp)
                    y_done.wait(sp, b - 1, 1)
                    sp.dma_start(z[:], mixed[p].rearrange("h s dd l -> (h s) (dd l)")).then_inc(o_done.sem, 16)
                if has(i + 1):
                    b, p = i + 1, 1 - par
                    parts.wait(sp, b, 2)
                    for side in range(2):
                        for r in range(3):
                            sp.dma_start(spill[p, side, r].rearrange("dd h n -> h dd n"),
                                         qkp[:, side, r]).then_inc(spilled.sem, 16)
                    spilled.wait(sp, b, 96)
                    for g in range(G):
                        stacked[g].wait(sp, b - 1, 96)
                        pv_done.wait(sp, i - 1, 16 * (g + 1))
                        for t0, n, part in TERM_RUNS:
                            heads = slice(g * G, (g + 1) * G)
                            sp.dma_start(QS[t0 * 8:(t0 + n) * 8, p, heads],
                                         spill[p, 0, part:part + 1, :, heads].rearrange("r dd h n -> r dd (h n)")
                                         .broadcast_to([n, DH8, G * S])).then_inc(stacked[g].sem, 16)
                            sp.dma_start(KS[t0 * 8:(t0 + n) * 8, p, heads],
                                         spill[p, 1, 0:n, :, heads].rearrange("r dd h n -> (r dd) h n")
                                         ).then_inc(stacked[g].sem, 16)
                if has(i):
                    m_parts.wait(sp, i, 1)
                    pv_done.wait(sp, i - 2, 64)
                    for r in range(3):
                        sp.dma_start(QS[MROW + r:MROW + r + 1, par], mparts[:, r]).then_inc(m_rows.sem, 16)
                if has(i - 1):
                    c_raw.wait(sp, i - 1, G)
                    inv_out.wait(sp, i - 2, 16)
                    sp.dma_start(comp[:], cn[DH8::32].rearrange("p g n -> p (g n)")).then_inc(sums_in.sem, 16)

            steps(sp, step)

        @block.tensor
        def _(pe):
            pe.wait_ge(loaded, 16 * LOADS)
            if w_sum:
                nc.tensor.matmul(PM[:, 0, 0:1], wo[:, 0], net.mean[:, 0:1], start=True, stop=True).then_inc(wsum_done, 1)
                pe.wait_ge(g_ready, 1)
            pe.wait_ge(filled, 5)

            def a_unit(b, par, u):
                g, t, j = UNITS[u]
                h, w = g * G + j, (P * (t + 1) if causal else S)
                maxed.wait(pe, b, u - 1)
                if u % 16 == 0:
                    stacked[g].wait(pe, b, 96)
                q = QS[0:MROW, par, h, t * P:(t + 1) * P]
                mm = nc.tensor.matmul(PA[:, u % 2, 0:w], q, KS[0:MROW, par, h, 0:w], start=True, stop=not causal)
                if causal:
                    mm = nc.tensor.matmul(PA[:, u % 2, t * P:w], net.ident_b[:], net.mask_qk[:], start=False, stop=True)
                mm.then_inc(a_done.sem, 1)

            def b_unit(b, par, u):
                g, t, j = UNITS[u]
                h, q0 = g * G + j, (P * t if causal else 0)
                exped.wait(pe, b, u - 1)
                if u == 0:
                    m_rows.wait(pe, b, 48)
                k = KS[:, par, h, t * P:(t + 1) * P]
                mm = nc.tensor.matmul(PB[:, u % 2, q0:S], k, QS[:, par, h, q0:S], start=True, stop=not causal)
                if causal:
                    mm = nc.tensor.matmul(PB[:, u % 2, q0:q0 + P], net.ident_b[:], net.mask_kq[:], start=False, stop=True)
                mm.then_inc(b_done.sem, 1)

            def pv_units(b, par, u):
                exped.wait(pe, b, u + G)
                for j in range(G):
                    g, t, _ = UNITS[u + j]
                    h, q0 = g * G + j, (P * t if causal else 0)
                    if (u + j) % 16 == 0:
                        c_raw.wait(pe, b, g - 1)
                    nc.tensor.matmul(PO[32 * j:32 * j + 32, g % 2, q0:S], V[:, par, t, h], prob[:, (u + j) % RING, q0:S],
                                     start=(t == 0), stop=(t == NT - 1), tile_position=(0, 32 * j)).then_inc(pv_done.sem, 1)

            def step(i, par):
                for v in range(64 + LEAD + LAG):
                    if v < 64 and has(i):
                        a_unit(i, par, v)
                    if LEAD <= v < 64 + LEAD and has(i - 1):
                        b_unit(i - 1, 1 - par, v - LEAD)
                    u = v - LEAD - LAG
                    if u % G == G - 1 and u > 0 and has(i - 1):
                        pv_units(i - 1, 1 - par, u - G + 1)
                    if v == O_PROJ and has(i - 2) and not w_sum:
                        if has(i + 1):
                            turned.wait(pe, i + 1, 2)
                        else:
                            y_done.wait(pe, i - 3, 1)
                        for g in range(G):
                            c_norm.wait(pe, i - 2, 1)
                            mm = nc.tensor.matmul(PM[:, 1], wo[:, g], cn[:, g], start=(g == 0), stop=(g == G - 1))
                        mm.then_inc(o_done.sem, 1)
                    if has(i + 1):
                        h = H[:, i + 1]
                        if v == Q_PROJ:
                            m_parts.wait(pe, i - 1, 1)
                            if not w_sum:
                                y_done.wait(pe, i - 3, 1)
                            mm = nc.tensor.matmul(PM[:, 0], wqk[:, 0], h, start=True, stop=True)
                            if rope:
                                mm = nc.tensor.matmul(PM[:, 1], wqk[:, 1], h, start=True, stop=True)
                            mm.then_inc(projected.sem, 1)
                        if v == K_PROJ:
                            turned.wait(pe, i + 1, 1)
                            mm = nc.tensor.matmul(PM[:, 0], wqk[:, NQK // 2], h, start=True, stop=True)
                            if rope:
                                mm = nc.tensor.matmul(PM[:, 1], wqk[:, 3], h, start=True, stop=True)
                            mm.then_inc(projected.sem, 1)
                    if v == V_PROJ and has(i):
                        m_parts.wait(pe, i - 1, 1)
                        if has(i + 1):
                            turned.wait(pe, i + 1, 2)
                        h_here.wait(pe, i, 1)
                        for t in range(NT):
                            mm = nc.tensor.matmul(PM[:, 0, t * P:(t + 1) * P], hcopy[:, t * P:(t + 1) * P], wv[:],
                                                  start=True, stop=True)
                        mm.then_inc(v_made.sem, 1)
                    if v == 66 and has(i):
                        v_ready.wait(pe, i, 1)
                        maxed.wait(pe, i, 64)
                        for t in range(NT):
                            tr = nc.tensor.transpose(PM[0:H16, 0, t * P:(t + 1) * P], neg[:, t], net.ident[:])
                        tr.then_inc(m_turned.sem, 1)

            steps(pe, step)

        @block.scalar
        def _(act):
            def step(i, par):
                if has(i):
                    v_made.wait(act, i - 1, 1)
                    nc.scalar.activation(hcopy[:], H[:, i], ACT.Copy).then_inc(h_here.sem, 1)
                b, p = i - 1, 1 - par

                def evacuate(g):
                    pv_done.wait(act, b, 16 * (g + 1))
                    if w_sum:
                        mixing.wait(act, b - 1, 16 * H16)
                    else:
                        o_done.wait(act, b - 1, 1)
                    nc.scalar.activation(cn[:, g], PO[:, g % 2], ACT.Copy).then_inc(c_raw.sem, 1)

                for u in range(64):
                    if has(b):
                        g, t, j = UNITS[u]
                        q0 = P * t if causal else 0
                        b_done.wait(act, b, u + 1)
                        pv_done.wait(act, b, u - RING + 1)
                        nc.scalar.activation(prob[:, u % RING, q0:S], PB[:, u % 2, q0:S], ACT.Exp,
                                             scale=scale).then_inc(exped.sem, 1)
                        if u % 16 == 14 and u > 16:
                            evacuate(u // 16 - 1)
                    if u == (44 if w_sum else 29) and has(i - 2):
                        c = i - 2
                        o_done.wait(act, c, o_done.per)
                        x_done.wait(act, c - 1, 1)
                        if w_sum:
                            nc.scalar.activation(y[:].rearrange("p (l dd) -> p l dd", dd=DH8),
                                                 z[:].rearrange("p (dd l) -> p l dd", dd=DH8), ACT.Copy,
                                                 scale=col(gbo, c)).then_inc(y_done.sem, 1)
                        else:
                            nc.scalar.activation(y[:], PM[:, 1], ACT.Identity, scale=col(gate, c),
                                                 bias=col(gbo, c)).then_inc(y_done.sem, 1)
                if has(b):
                    evacuate(G - 1)

            steps(act, step)

        @block.gpsimd
        def _(pool):
            nc.gpsimd.memset(QS[:].bitcast(U32), 0).then_inc(filled, 1)
            nc.gpsimd.memset(V[:], 1.0).then_inc(filled, 1)
            pool.sem_inc(x_done.sem, x_done.credit)

            def add(b):
                y_done.wait(pool, b, 1)
                x = X[:, b]
                nc.gpsimd.tensor_tensor(x, x, y[:], ALU.add).then_inc(x_done.sem, 1)

            def normalise(b):
                inv_in.wait(pool, b, 64)
                nc.gpsimd.tensor_tensor(cn[:], cn[:], rs[:], ALU.mult).then_inc(c_norm.sem, 1)

            def step(i, par):
                if w_sum and has(i - 2):
                    normalise(i - 2)
                if has(i + 1):
                    b = i + 1
                    part_chain.start(b)
                    for side in range(2):
                        turned.wait(pool, b, side + 1)
                        if side == 0:
                            spilled.wait(pool, b - 1, 96)
                        q, pt = qk[:, side], qkp[:, side]
                        stand_alone(net, pool)
                        part_chain.link(pool, nc.gpsimd.tensor_copy(pt[:, 0], q))
                        part_chain.link(pool, nc.gpsimd.tensor_tensor(q, q, pt[:, 0], ALU.subtract))
                        stand_alone(net, pool)
                        part_chain.link(pool, nc.gpsimd.tensor_copy(pt[:, 1], q))
                        nc.gpsimd.tensor_tensor(pt[:, 2], q, pt[:, 1], ALU.subtract).then_inc(parts.sem, 1)
                if has(i - 2):
                    if not w_sum:
                        normalise(i - 2)
                    add(i - 2)

            steps(pool, step)

        @block.vector
        def _(dve):
            nc.vector.memset(KS[0:MROW].bitcast(U32), 0).then_inc(filled, 1)
            nc.vector.memset(KS[MROW:P], 1.0).then_inc(filled, 1)
            dve.wait_ge(loaded, 16 * LOADS)
            if w_sum:
                dve.wait_ge(wsum_done, 1)
                nc.vector.tensor_scalar(gbo[:], gate, PM[:, 0, 0:1], float(P), ALU.mult, ALU.mult).then_inc(g_ready, 1)
                dve.wait_ge(g_ready, 1)
            else:
                nc.vector.tensor_scalar(gbo[:], gate, bo[:, 0:1], None, ALU.mult).then_inc(g_ready, 1)
                dve.wait_ge(g_ready, 1)
            nc.vector.memset(rs[:], 1.0).then_inc(filled, 1)

            def lay_out(b, side):
                parts.wait(dve, b - 1, 2)
                projected.wait(dve, b, side + 1)
                if rope:
                    turn_chain.link(dve, nc.vector.scalar_tensor_tensor(
                        qk[:, side], PM[:, 0], bqk[:, 2 * side:2 * side + 1], turn[:, 0], ALU.add, ALU.mult))
                    turn_chain.link(dve, nc.vector.scalar_tensor_tensor(
                        t2[:], PM[:, 1], bqk[:, 2 * side + 1:2 * side + 2], turn[:, 1], ALU.add, ALU.mult))
                    nc.vector.tensor_tensor(qk[:, side], qk[:, side], t2[:], ALU.add).then_inc(turned.sem, 1)
                    turned.wait(dve, b, side + 1)
                else:
                    nc.vector.tensor_copy(qk[:, side], PM[:, 0]).then_inc(turned.sem, 1)

            def step(i, par):
                if has(i + 1):
                    turn_chain.start(i + 1)
                for v in range(64):
                    if has(i):
                        g, t, j = UNITS[v]
                        w = P * (t + 1) if causal else S
                        a_done.wait(dve, i, v + 1)
                        nc.vector.tensor_reduce(neg[:, t, g * G + j:g * G + j + 1], PA[:, v % 2, 0:w], AX,
                                                ALU.max, negate=True).then_inc(maxed.sem, 1)
                    if has(i + 1):
                        if v == Q_PROJ + 2:
                            lay_out(i + 1, 0)
                        if v == K_PROJ + 2:
                            lay_out(i + 1, 1)
                    if v == 6 and has(i - 2):
                        sums_in.wait(dve, i - 2, 16)
                        nc.vector.reciprocal(comp[:], comp[:]).then_inc(inverted.sem, 1)
                    if v == V_PROJ + 2 and has(i):
                        v_made.wait(dve, i, 1)
                        pv_done.wait(dve, i - 2, 64)
                        vout(i, par)
                if has(i):
                    m_chain.start(i)
                    m_turned.wait(dve, i, 1)
                    m_rows.wait(dve, i - 1, 48)
                    m = PM[0:H16, 0]
                    m_chain.link(dve, nc.vector.tensor_copy(mparts[:, 0], m))
                    m_chain.link(dve, nc.vector.tensor_tensor(mres[:], m, mparts[:, 0], ALU.subtract))
                    m_chain.link(dve, nc.vector.tensor_copy(mparts[:, 1], mres[:]))
                    nc.vector.tensor_tensor(mparts[:, 2], mres[:], mparts[:, 1], ALU.subtract).then_inc(m_parts.sem, 1)

            def vout(b, par):
                out = V[:, par, :, :, 0:DH8]
                src = PM[:, 0].rearrange("p (t h dd) -> p t h dd", t=NT, dd=DH8)
                for t in range(NT):
                    if w_sum:
                        ins = nc.vector.tensor_copy(out[:, t], src[:, t])
                    else:
                        ins = nc.vector.tensor_tensor(out[:, t], src[:, t],
                                                      bv[:].rearrange("p (h dd) -> p h dd", dd=DH8), ALU.add)
                ins.then_inc(v_ready.sem, 1)

            steps(dve, step)


F4 = 4
E8 = 8


def softmax_top2(nc, dve, link, wait_exp, logits, mx, p, ssum, best, index, pair, n):
    link(nc.vector.tensor_reduce(mx, logits, AX, ALU.max))
    link(nc.vector.tensor_tensor(p, logits, mx.unsqueeze(2).broadcast_to([mx.shape[0], n, E8]), ALU.subtract))
    wait_exp()
    link(nc.vector.tensor_reduce(ssum, p, AX, ALU.add))
    link(nc.vector.reciprocal(ssum, ssum))
    link(nc.vector.tensor_tensor(p, p, ssum.unsqueeze(2).broadcast_to([mx.shape[0], n, E8]), ALU.mult))
    for t in range(n):
        link(nc.vector.max(best[:, t], p[:, t]))
        link(nc.vector.max_index(index[:, t], best[:, t], p[:, t]))
    link(nc.vector.tensor_reduce(ssum, best[:, :, 0:2], AX, ALU.add))
    link(nc.vector.reciprocal(ssum, ssum))
    link(nc.vector.tensor_tensor(pair, best[:, :, 0:2], ssum.unsqueeze(2).broadcast_to([mx.shape[0], n, 2]), ALU.mult))


def route_batches_phase(net):
    nc, d = net.nc, net.d
    with ExitStack() as ctx:
        def sb(n, shape, dt=F32):
            return ctx.enter_context(nc.sbuf_tensor("r0_" + n, shape, dt))

        hm = sb("hm", [P, B])
        wg = sb("wg", [P, E8])
        bg = sb("bg", [B, 1, E8])
        alpha = sb("alpha", [B, 1])
        rest = sb("rest", [B, 1])
        lg = sb("lg", [B, 1, E8])
        p = sb("p", [B, 1, E8])
        mx = sb("mx", [B, 1])
        ssum = sb("ssum", [B, 1])
        best = sb("best", [B, 1, E8])
        index = sb("index", [B, 1, E8], U32)
        pair = sb("pair", [B, 1, 2])
        w = sb("w", [B, 3])
        ps = ctx.enter_context(nc.psum_tensor("r0_ps", [P, S], F32))
        w_dram = nc.dram_tensor("r0_w_dram", [B, 3], F32, kind="Internal").ap()
        i_dram = nc.dram_tensor("r0_i_dram", [B, 2], U32, kind="Internal").ap()
        loaded = nc.alloc_semaphore("r0_loaded")
        means = nc.alloc_semaphore("r0_means")
        logit = nc.alloc_semaphore("r0_logit")
        less_max = nc.alloc_semaphore("r0_less_max")
        exped = nc.alloc_semaphore("r0_exped")
        routed = nc.alloc_semaphore("r0_routed")
        out1 = nc.alloc_semaphore("r0_out1")
        out2 = nc.alloc_semaphore("r0_out2")
        ch = nc.alloc_semaphore("r0_chain")
        block = ctx.enter_context(nc.Block())

        @block.sync
        def _(sp):
            sp.dma_start(wg[:], d["f0_wg"]).then_inc(loaded, 16)
            sp.dma_start(bg[:, 0], d["f0_bg"].partition_broadcast(B)).then_inc(loaded, 16)
            sp.dma_start(alpha[:], d["f0_alpha"].partition_broadcast(B)).then_inc(loaded, 16)
            sp.wait_ge(routed, 1)
            sp.dma_start(w_dram, w[:]).then_inc(out1, 16)
            sp.dma_start(i_dram, index[:, 0, 0:2]).then_inc(out1, 16)
            sp.wait_ge(out1, 32)
            sp.dma_start(net.w3[:], w_dram.rearrange("b k -> (b k)").partition_broadcast(P)).then_inc(out2, 16)
            sp.dma_start(net.chosen[:], i_dram.rearrange("b (k o) -> o (b k)", o=1)).then_inc(out2, 16)
            sp.wait_ge(out2, 32)

        @block.tensor
        def _(pe):
            pe.wait_ge(loaded, 48)
            pe.wait_ge(means, 2)
            nc.tensor.matmul(ps[0:B, 0:E8], hm[:], wg[:], start=True, stop=True).then_inc(logit, 1)

        @block.scalar
        def _(act):
            act.wait_ge(less_max, 1)
            nc.scalar.activation(p[:], p[:], ACT.Exp).then_inc(exped, 1)

        @block.vector
        def _(dve):
            n = [0]

            def link(ins):
                n[0] += 1
                ins.then_inc(ch, 1)
                dve.wait_ge(ch, n[0])

            nc.vector.tensor_reduce(hm[:], net.H[:], AX, ALU.add).then_inc(means, 1)
            dve.wait_ge(means, 1)
            nc.vector.tensor_scalar(hm[:], hm[:], 1.0 / S, None, ALU.mult).then_inc(means, 1)
            dve.wait_ge(logit, 1)
            link(nc.vector.tensor_tensor(lg[:, 0], ps[0:B, 0:E8], bg[:, 0], ALU.add))

            def wait_exp():
                dve.sem_inc(less_max, 1)
                dve.wait_ge(exped, 1)

            softmax_top2(nc, dve, link, wait_exp, lg[:], mx[:], p[:], ssum[:], best[:], index[:], pair[:], 1)
            link(nc.vector.tensor_scalar(w[:, 0:1], alpha[:], 0.1, 1.0, ALU.max, ALU.min))
            link(nc.vector.tensor_scalar(rest[:], w[:, 0:1], -1.0, 1.0, ALU.mult, ALU.add))
            nc.vector.tensor_scalar(w[:, 1:3], pair[:, 0], rest[:, 0:1], None, ALU.mult).then_inc(routed, 1)


def mlp_phase(net, name, layer, NU, dynamic):
    nc, X, H, d = net.nc, net.X, net.H, net.d
    gate = net.MOD[:, layer, 5]
    NW = 3 if dynamic else NU
    with ExitStack() as ctx:
        def sb(n, shape, dt=F32):
            return ctx.enter_context(nc.sbuf_tensor(name + n, shape, dt))

        w1 = sb("w1", [P, NW, F4 * P])
        w2 = sb("w2", [P, NW, F4, P])
        bias = sb("bias", [P, NW, F4 + 1])
        hid = sb("hid", [P, 2, F4, S])
        t = sb("t", [P, S])
        wt = None if dynamic else sb("wt", [P, 2, E8, S])
        ph = ctx.enter_context(nc.psum_tensor(name + "ph", [P, F4, S], F32))
        po = ctx.enter_context(nc.psum_tensor(name + "po", [P, 2, S], F32))
        loaded = nc.alloc_semaphore(name + "loaded")
        fetched = [Signal(ctx, nc, f"{name}fetched{k}", 48) for k in range(2)]
        spread = Signal(ctx, nc, name + "spread", 16)
        fc = Signal(ctx, nc, name + "fc", F4 * NU)
        act_done = Signal(ctx, nc, name + "act_done", F4 * NU)
        proj = Signal(ctx, nc, name + "proj", NU)
        weighed = Signal(ctx, nc, name + "weighed", NU)
        added = Signal(ctx, nc, name + "added", NU)
        block = ctx.enter_context(nc.Block())

        def batches(eng, batch):
            batch(0, 0)
            batch(1, 1)
            with eng.Fori(1, B // 2) as pair:
                batch(pair * 2, 0)
                batch(pair * 2 + 1, 1)

        @block.sync
        def _(sp):
            if dynamic:
                sp.dma_start(w1[:, 0], d[name + "w1m"]).then_inc(loaded, 16)
                sp.dma_start(w2[:, 0], d[name + "w2m"].rearrange("(t p) n -> p t n", p=P)).then_inc(loaded, 16)
                sp.dma_start(bias[:, 0], d[name + "bm"]).then_inc(loaded, 16)

                def batch(b, par):
                    for k in range(2):
                        proj.wait(sp, b - 1, k + 2)
                        added.wait(sp, b - 1, k + 2)
                        e = sp.value_load(net.chosen[0:1, bass.ds(b * 2 + k, 1)], min_val=0, max_val=E8 - 1)
                        sp.dma_start(w1[:, 1 + k], d[name + "w1e"][bass.ds(e, 1)].rearrange("o p n -> (o p) n")).then_inc(fetched[k].sem, 16)
                        sp.dma_start(w2[:, 1 + k], d[name + "w2e"][bass.ds(e, 1)].rearrange("o (t p) n -> (o p) t n", p=P)
                                     ).then_inc(fetched[k].sem, 16)
                        sp.dma_start(bias[:, 1 + k], d[name + "be"][bass.ds(e, 1)].rearrange("o p n -> (o p) n")).then_inc(fetched[k].sem, 16)
                batches(sp, batch)
            else:
                for u in range(NU):
                    sp.dma_start(w1[:, u], d[name + "w1"][u]).then_inc(loaded, 16)
                    sp.dma_start(w2[:, u], d[name + "w2"][u].rearrange("(t p) n -> p t n", p=P)).then_inc(loaded, 16)
                sp.dma_start(bias[:], d[name + "b"].rearrange("u p n -> p u n")).then_inc(loaded, 16)

                def batch(b, par):
                    added.wait(sp, b - 2, NU)
                    spread.wait(sp, b - 1, 16)
                    sp.dma_start(wt[:, par], net.gate_dram[bass.ds(b, 1)].rearrange("o e n -> (o e n)").partition_broadcast(P)
                                 ).then_inc(spread.sem, 16)
                for b in range(4):
                    batch(b, b % 2)
                with sp.Fori(2, B // 2) as pair:
                    batch(pair * 2, 0)
                    batch(pair * 2 + 1, 1)

        @block.tensor
        def _(pe):
            pe.wait_ge(loaded, 48 if dynamic else 16 * (2 * NU + 1))

            def up(b, par, u):
                if dynamic and u:
                    fetched[u - 1].wait(pe, b, 48)
                for k in range(F4):
                    act_done.wait(pe, b, F4 * (u - 1) + k + 1)
                    nc.tensor.matmul(ph[:, k], w1[:, u, k * P:(k + 1) * P], H[:, b], start=True, stop=True).then_inc(fc.sem, 1)

            def down(b, par, u):
                slot = (par * NU + u) % 2
                weighed.wait(pe, b, u - 1)
                for k in range(F4):
                    act_done.wait(pe, b, F4 * u + k + 1)
                    mm = nc.tensor.matmul(po[:, slot], w2[:, u, k], hid[:, slot, k], start=(k == 0), stop=(k == F4 - 1))
                mm.then_inc(proj.sem, 1)

            def batch(b, par):
                for u in range(NU):
                    up(b, par, u)
                    if u:
                        down(b, par, u - 1)
                    elif not (isinstance(b, int) and b == 0):
                        down(b - 1, 1 - par, NU - 1)
            batches(pe, batch)
            down(B - 1, 1, NU - 1)

        @block.scalar
        def _(act):
            act.wait_ge(loaded, 48 if dynamic else 16 * (2 * NU + 1))

            def batch(b, par):
                for u in range(NU):
                    slot = (par * NU + u) % 2
                    proj.wait(act, b, u - 1)
                    if dynamic and u:
                        fetched[u - 1].wait(act, b, 48)
                    for k in range(F4):
                        fc.wait(act, b, F4 * u + k + 1)
                        nc.scalar.activation(hid[:, slot, k], ph[:, k], ACT.Gelu_apprx_tanh,
                                             bias=bias[:, u, k:k + 1]).then_inc(act_done.sem, 1)
            batches(act, batch)

        @block.vector
        def _(dve):
            dve.wait_ge(loaded, 48 if dynamic else 16 * (2 * NU + 1))

            def batch(b, par):
                for u in range(NU):
                    slot = (par * NU + u) % 2
                    if dynamic and u:
                        fetched[u - 1].wait(dve, b, 48)
                    proj.wait(dve, b, u + 1)
                    added.wait(dve, b, u)
                    b2 = bias[:, u, F4:F4 + 1]
                    if dynamic:
                        ins = nc.vector.tensor_scalar(t[:], po[:, slot], b2, net.w3[:, bass.ds(b * 3 + u, 1)], ALU.add, ALU.mult)
                    elif u == 0:
                        spread.wait(dve, b, 16)
                        ins = nc.vector.tensor_scalar(t[:], po[:, slot], b2, None, ALU.add)
                    else:
                        ins = nc.vector.scalar_tensor_tensor(t[:], po[:, slot], b2, wt[:, par, u - 1], ALU.add, ALU.mult)
                    ins.then_inc(weighed.sem, 1)
                    weighed.wait(dve, b, u + 1)
                    nc.vector.scalar_tensor_tensor(X[:, b], t[:], col(gate, b), X[:, b], ALU.mult, ALU.add).then_inc(added.sem, 1)
            batches(dve, batch)


def wide_head_phase(net, name, layer):
    nc, X, H, d = net.nc, net.X, net.H, net.d
    gate = net.MOD[:, layer, 2]
    scale = float(P ** -0.5)
    with ExitStack() as ctx:
        def sb(n, shape, dt=F32):
            return ctx.enter_context(nc.sbuf_tensor(name + n, shape, dt))

        def psum(n, shape):
            return ctx.enter_context(nc.psum_tensor(name + n, shape, F32))

        def sig(n, per):
            return Signal(ctx, nc, name + n, per)

        w = sb("w", [P, 4, P])
        hc = sb("hc", [P, S])
        q, k = sb("q", [P, S]), sb("k", [P, S])
        v = sb("v", [P, 2, NT, P])
        neg, bias, total, inv = (sb(n, [P, 2, NT]) for n in ("neg", "bias", "total", "inv"))
        prob = sb("prob", [P, 2, NT, S])
        pt = sb("pt", [P, NT, S])
        c = sb("c", [P, S])
        PJ, PA, PT, PO = (psum(n, [P, 2, S]) for n in ("PJ", "PA", "PT", "PO"))
        loaded = nc.alloc_semaphore(name + "loaded")
        h_here = sig("h_here", 1)
        proj = sig("proj", 2)
        q_out, v_out, k_out = sig("q_out", 1), sig("v_out", 1), sig("k_out", 1)
        scored = sig("scored", NT)
        maxed = sig("maxed", 2 * NT)
        exped = sig("exped", NT)
        normed = sig("normed", 2 * NT)
        t_done = sig("t_done", NT)
        t_out = sig("t_out", NT)
        pv = sig("pv", 1)
        c_out = sig("c_out", 1)
        o_done = sig("o_done", 1)
        x_done = sig("x_done", 1)
        block = ctx.enter_context(nc.Block())

        def batches(eng, front, back):
            front(0, 0)
            front(1, 1)
            back(0, 0)
            with eng.Fori(1, B // 2) as pair:
                for par in range(2):
                    front(pair * 2 + par, par)
                    back(pair * 2 + (par - 1), 1 - par)
            back(B - 1, 1)

        @block.sync
        def _(sp):
            sp.dma_start(w[:], d[name + "w"].rearrange("j p n -> p j n")).then_inc(loaded, 16)

        @block.tensor
        def _(pe):
            pe.wait_ge(loaded, 16)

            def front(b, par):
                v_out.wait(pe, b - 1, 1)
                k_out.wait(pe, b - 1, 1)
                nc.tensor.matmul(PJ[:, 0], w[:, 0], H[:, b], start=True, stop=True)
                nc.tensor.matmul(PJ[:, 1], w[:, 1], H[:, b], start=True, stop=True).then_inc(proj.sem, 1)
                h_here.wait(pe, b, 1)
                q_out.wait(pe, b, 1)
                for t in range(NT):
                    mm = nc.tensor.matmul(PJ[:, 0, t * P:(t + 1) * P], hc[:, t * P:(t + 1) * P], w[:, 2], start=True, stop=True)
                mm.then_inc(proj.sem, 1)
                k_out.wait(pe, b, 1)
                for t in range(NT):
                    exped.wait(pe, b, t - 1)
                    nc.tensor.matmul(PA[:, t % 2, 0:(t + 1) * P], q[:, t * P:(t + 1) * P], k[:, 0:(t + 1) * P], start=True, stop=False)
                    nc.tensor.matmul(PA[:, t % 2, t * P:(t + 1) * P], net.ident_b[:], net.mask_qk[:], start=False, stop=True
                                     ).then_inc(scored.sem, 1)

            def back(b, par):
                for t in range(NT):
                    t_out.wait(pe, b, t - 1)
                    normed.wait(pe, b, 2 * NT)
                    for u in range(t, NT):
                        tr = nc.tensor.transpose(PT[:, t % 2, u * P:(u + 1) * P], prob[:, par, u, t * P:(t + 1) * P], net.ident[:])
                    tr.then_inc(t_done.sem, 1)
                for t in range(NT):
                    t_out.wait(pe, b, t + 1)
                    mm = nc.tensor.matmul(PO[:, 0, t * P:S], v[:, par, t], pt[:, t, t * P:S], start=(t == 0), stop=(t == NT - 1))
                mm.then_inc(pv.sem, 1)
                c_out.wait(pe, b, 1)
                x_done.wait(pe, b - 1, 1)
                nc.tensor.matmul(PO[:, 1], w[:, 3], c[:], start=True, stop=True).then_inc(o_done.sem, 1)
            batches(pe, front, back)

        @block.scalar
        def _(act):
            def front(b, par):
                proj.wait(act, b - 1, 2)
                nc.scalar.activation(hc[:], H[:, b], ACT.Copy).then_inc(h_here.sem, 1)
                proj.wait(act, b, 1)
                scored.wait(act, b - 1, NT)
                nc.scalar.activation(q[:], PJ[:, 0], ACT.Copy).then_inc(q_out.sem, 1)
                proj.wait(act, b, 2)
                pv.wait(act, b - 2, 1)
                nc.scalar.activation(v[:, par].rearrange("p t n -> p (t n)"), PJ[:, 0], ACT.Copy).then_inc(v_out.sem, 1)
                for t in range(NT):
                    maxed.wait(act, b, 2 * t + 2)
                    t_done.wait(act, b - 2, NT)
                    nc.scalar.activation(prob[:, par, t, 0:(t + 1) * P], PA[:, t % 2, 0:(t + 1) * P], ACT.Exp, scale=scale,
                                         bias=bias[:, par, t:t + 1], accum_out=total[:, par, t:t + 1]).then_inc(exped.sem, 1)

            def back(b, par):
                pv.wait(act, b, 1)
                o_done.wait(act, b - 1, 1)
                nc.scalar.activation(c[:], PO[:, 0], ACT.Copy).then_inc(c_out.sem, 1)

            for b in range(3):
                front(b, b % 2)
                if b:
                    back(b - 1, (b - 1) % 2)
            front(3, 1)
            back(2, 0)
            with act.Fori(2, B // 2) as pair:
                for par in range(2):
                    front(pair * 2 + par, par)
                    back(pair * 2 + (par - 1), 1 - par)
            back(B - 1, 1)

        @block.vector
        def _(dve):
            def front(b, par):
                proj.wait(dve, b, 1)
                scored.wait(dve, b - 1, NT)
                nc.vector.tensor_copy(k[:], PJ[:, 1]).then_inc(k_out.sem, 1)
                for t in range(NT):
                    scored.wait(dve, b, t + 1)
                    exped.wait(dve, b - 1, NT)
                    nc.vector.tensor_reduce(neg[:, par, t:t + 1], PA[:, t % 2, 0:(t + 1) * P], AX, ALU.max, negate=True
                                            ).then_inc(maxed.sem, 1)
                    maxed.wait(dve, b, 2 * t + 1)
                    nc.vector.tensor_scalar(bias[:, par, t:t + 1], neg[:, par, t:t + 1], scale, None, ALU.mult
                                            ).then_inc(maxed.sem, 1)
                for t in range(NT):
                    exped.wait(dve, b, t + 1)
                    nc.vector.reciprocal(inv[:, par, t:t + 1], total[:, par, t:t + 1]).then_inc(normed.sem, 1)
                    normed.wait(dve, b, 2 * t + 1)
                    pr = prob[:, par, t, 0:(t + 1) * P]
                    nc.vector.tensor_scalar(pr, pr, inv[:, par, t:t + 1], None, ALU.mult).then_inc(normed.sem, 1)

            def back(b, par):
                for t in range(NT):
                    t_done.wait(dve, b, t + 1)
                    pv.wait(dve, b - 1, 1)
                    nc.vector.tensor_copy(pt[:, t, t * P:S], PT[:, t % 2, t * P:S]).then_inc(t_out.sem, 1)
                o_done.wait(dve, b, 1)
                nc.vector.scalar_tensor_tensor(X[:, b], PO[:, 1], col(gate, b), X[:, b], ALU.mult, ALU.add).then_inc(x_done.sem, 1)
            front(0, 0)
            front(1, 1)
            back(0, 0)
            front(2, 0)
            back(1, 1)
            front(3, 1)
            back(2, 0)
            with dve.Fori(2, B // 2) as pair:
                for par in range(2):
                    front(pair * 2 + par, par)
                    back(pair * 2 + (par - 1), 1 - par)
            back(B - 1, 1)


E128, CAP = 128, 32
TT = B * NT
SKIP = 1 << 20


def bcast(ap, n):
    return ap.unsqueeze(2).broadcast_to([ap.shape[0], ap.shape[1], n])


def route_slots_phase(net):
    nc, d, H = net.nc, net.d, net.H
    with ExitStack() as ctx:
        def sb(n, shape, dt=F32):
            return ctx.enter_context(nc.sbuf_tensor("r2_" + n, shape, dt))

        def sem(n):
            return nc.alloc_semaphore("r2_" + n)

        wg = sb("wg", [P, E128])
        kf = sb("kf", [P, 2, P])
        tri, ones = sb("tri", [P, P], BF16), sb("ones", [P, P], BF16)
        LG = sb("LG", [P, TT, E128])
        M = sb("M", [P, 2, TT, E128], BF16)
        before = sb("before", [P, 2, TT + 1, E128], BF16)
        best = sb("best", [P, TT, 8])
        index = sb("index", [P, TT, 8], U32)
        idxf = sb("idxf", [P, 2, TT])
        tot = sb("tot", [P, TT])
        g2 = sb("g2", [P, TT])
        den = sb("den", [P, TT])
        loc = sb("loc", [P, 2, TT])
        over = sb("over", [P, 2, TT])
        own = sb("own", [P, 4, E128])
        PL = ctx.enter_context(nc.psum_tensor("r2_PL", [P, 4, 4, E128], F32))
        PR = ctx.enter_context(nc.psum_tensor("r2_PR", [P, 4, 4, E128], F32))
        loaded, logits, lg_out, less_max, exped = sem("loaded"), sem("logits"), sem("lg_out"), sem("less_max"), sem("exped")
        hot, summed, ranks, used, consts, done = sem("hot"), sem("summed"), sem("ranks"), sem("used"), sem("consts"), sem("done")
        small_exp, small_done = sem("small_exp"), sem("small_done")
        ch = sem("chain")
        block = ctx.enter_context(nc.Block())
        NG = TT // 4

        @block.sync
        def _(sp):
            sp.dma_start(wg[:], d["f2_wg"]).then_inc(loaded, 16)
            sp.dma_start(kf[:], d["k_route"].rearrange("a p n -> p a n")).then_inc(loaded, 16)

        @block.tensor
        def _(pe):
            pe.wait_ge(loaded, 32)
            for n in range(TT):
                g = n // 4
                if n % 4 == 0 and g >= 4:
                    pe.wait_ge(lg_out, g - 3)
                mm = nc.tensor.matmul(PL[:, g % 4, n % 4], H[:, n // NT, (n % NT) * P:(n % NT + 1) * P], wg[:], start=True, stop=True)
                if n % 4 == 3:
                    mm.then_inc(logits, 1)
            pe.wait_ge(consts, 2)
            for c in range(2):
                for g in range(NG):
                    G_ = c * NG + g
                    pe.wait_ge(summed, 1 + 4 * G_ + 4)
                    pe.wait_ge(hot, G_ + 1 if c == 0 else NG + g + 1)
                    if G_ >= 4:
                        pe.wait_ge(used, G_ - 3)
                    for j in range(4):
                        n = 4 * g + j
                        nc.tensor.matmul(PR[:, G_ % 4, j], ones[:], before[:, c, n], start=True, stop=False)
                        mm = nc.tensor.matmul(PR[:, G_ % 4, j], tri[:], M[:, c, n], start=False, stop=True)
                    mm.then_inc(ranks, 1)

        @block.scalar
        def _(act):
            for g in range(NG):
                act.wait_ge(logits, g + 1)
                nc.scalar.activation(LG[:, 4 * g:4 * g + 4], PL[:, g % 4], ACT.Copy).then_inc(lg_out, 1)
            for g in range(NG):
                act.wait_ge(less_max, g + 1)
                lg = LG[:, 4 * g:4 * g + 4]
                nc.scalar.activation(lg, lg, ACT.Exp).then_inc(exped, 1)
            act.wait_ge(small_exp, 1)
            nc.scalar.activation(g2[:], g2[:], ACT.Exp).then_inc(small_done, 1)

        @block.gpsimd
        def _(pool):
            nc.gpsimd.memset(before[:, 0, 0], 0.0).then_inc(summed, 1)
            for c in range(2):
                if c == 1:
                    pool.wait_ge(summed, TT + 1)
                    nc.gpsimd.tensor_copy(before[:, 1, 0], before[:, 0, TT]).then_inc(summed, 1)
                for n in range(TT):
                    if n % 4 == 0:
                        pool.wait_ge(hot, c * NG + n // 4 + 1)
                    k = c * (TT + 1) + n + 1
                    pool.wait_ge(summed, k)
                    nc.gpsimd.tensor_tensor(before[:, c, n + 1], before[:, c, n], M[:, c, n], ALU.add).then_inc(summed, 1)

        @block.vector
        def _(dve):
            k = [0]

            def link(ins):
                k[0] += 1
                ins.then_inc(ch, 1)
                dve.wait_ge(ch, k[0])

            dve.wait_ge(loaded, 32)
            nc.vector.tensor_copy(tri[:], kf[:, 0]).then_inc(consts, 1)
            nc.vector.memset(ones[:], 1.0).then_inc(consts, 1)
            iota = kf[:, 1].unsqueeze(1).broadcast_to([P, 4, E128])
            for g in range(NG):
                t4 = slice(4 * g, 4 * g + 4)
                dve.wait_ge(lg_out, g + 1)
                for n in range(4 * g, 4 * g + 4):
                    link(nc.vector.max(best[:, n], LG[:, n]))
                for n in range(4 * g, 4 * g + 4):
                    link(nc.vector.max_index(index[:, n], best[:, n], LG[:, n]))
                for c in range(2):
                    link(nc.vector.tensor_copy(idxf[:, c, t4], index[:, t4, c]))
                nc.vector.tensor_tensor(M[:, 0, t4], iota, bcast(idxf[:, 0, t4], E128), ALU.is_equal).then_inc(hot, 1)
                nc.vector.tensor_tensor(LG[:, t4], LG[:, t4], bcast(best[:, t4, 0], E128), ALU.subtract).then_inc(less_max, 1)
            for g in range(NG):
                t4 = slice(4 * g, 4 * g + 4)
                nc.vector.tensor_tensor(M[:, 1, t4], iota, bcast(idxf[:, 1, t4], E128), ALU.is_equal).then_inc(hot, 1)
            for g in range(NG):
                dve.wait_ge(exped, g + 1)
                link(nc.vector.tensor_reduce(tot[:, 4 * g:4 * g + 4], LG[:, 4 * g:4 * g + 4], AX, ALU.add))
            nc.vector.tensor_tensor(g2[:], best[:, :, 1], best[:, :, 0], ALU.subtract).then_inc(small_exp, 1)
            link(nc.vector.reciprocal(tot[:], tot[:]))
            dve.wait_ge(small_done, 1)
            link(nc.vector.tensor_tensor(g2[:], g2[:], tot[:], ALU.mult))
            link(nc.vector.tensor_tensor(den[:], g2[:], tot[:], ALU.add))
            link(nc.vector.tensor_scalar(den[:], den[:], float(np.finfo(np.float32).eps), None, ALU.max))
            link(nc.vector.reciprocal(den[:], den[:]))
            for c in range(2):
                for g in range(NG):
                    t4 = slice(4 * g, 4 * g + 4)
                    G_ = c * NG + g
                    dve.wait_ge(ranks, G_ + 1)
                    nc.vector.tensor_tensor(own[:], PR[:, G_ % 4], M[:, c, t4], ALU.mult).then_inc(used, 1)
                    dve.wait_ge(used, G_ + 1)
                    link(nc.vector.tensor_reduce(loc[:, c, t4], own[:], AX, ALU.add))
            link(nc.vector.tensor_scalar(over[:], loc[:], float(CAP), None, ALU.is_ge))
            link(nc.vector.scalar_tensor_tensor(loc[:], idxf[:], float(CAP), loc[:], ALU.mult, ALU.add))
            link(nc.vector.scalar_tensor_tensor(loc[:], over[:], float(SKIP), loc[:], ALU.mult, ALU.add))
            link(nc.vector.tensor_copy(net.slot[:], loc[:]))
            link(nc.vector.tensor_scalar(over[:], over[:], -1.0, 1.0, ALU.mult, ALU.add))
            for c, g in ((0, tot), (1, g2)):
                link(nc.vector.tensor_tensor(g[:], g[:], den[:], ALU.mult))
                link(nc.vector.tensor_tensor(net.wgt[:, c], g[:], over[:, c], ALU.mult))


def dispatch_phase(net):
    nc, H = net.nc, net.H
    with ExitStack() as ctx:
        R = 4
        rows = ctx.enter_context(nc.sbuf_tensor("d2_rows", [P, R, P], F32))
        zero = ctx.enter_context(nc.sbuf_tensor("d2_zero", [P, 1024], F32))
        pt = ctx.enter_context(nc.psum_tensor("d2_pt", [P, 2, S], F32))
        turned, copied, zeroed, cleared = (nc.alloc_semaphore("d2_" + n) for n in
                                           ("turned", "copied", "zeroed", "cleared"))
        sent = [nc.alloc_semaphore(f"d2_sent{r}") for r in range(R)]
        block = ctx.enter_context(nc.Block())

        @block.sync
        def _(sp):
            sp.wait_ge(zeroed, 1)
            flat = net.buf.rearrange("(p r) n -> p (r n)", p=P)
            for i in range(4):
                sp.dma_start(flat[:, i * 1024:(i + 1) * 1024], zero[:]).then_inc(cleared, 16)

        @block.tensor
        def _(pe):
            for n in range(TT):
                if n >= 2:
                    pe.wait_ge(copied, n - 1)
                nc.tensor.transpose(pt[:, n % 2, 0:P], H[:, n // NT, (n % NT) * P:(n % NT + 1) * P], net.ident[:]).then_inc(turned, 1)

        @block.vector
        def _(dve):
            nc.vector.memset(zero[:], 0.0).then_inc(zeroed, 1)
            for n in range(TT):
                dve.wait_ge(turned, n + 1)
                if n >= R:
                    dve.wait_ge(sent[n % R], 32 * (n // R))
                nc.vector.tensor_copy(rows[:, n % R], pt[:, n % 2, 0:P]).then_inc(copied, 1)

        @block.gpsimd
        def _(pool):
            pool.wait_ge(cleared, 64)
            for n in range(TT):
                pool.wait_ge(copied, n + 1)
                for c in range(2):
                    nc.gpsimd.indirect_dma_start(
                        out=net.buf, out_offset=bass.IndirectOffsetOnAxis(ap=net.slot[:, c, n:n + 1], axis=0),
                        in_=rows[:, n % R], in_offset=None, bounds_check=E128 * CAP - 1, oob_is_err=False,
                    ).then_inc(sent[n % R], 16)
            for r in range(R):
                pool.wait_ge(sent[r], 32 * (TT // R))


def experts_phase(net):
    nc, d = net.nc, net.d
    C, R = E128 // 4, 4
    with ExitStack() as ctx:
        def sb(n, shape, dt=F32):
            return ctx.enter_context(nc.sbuf_tensor("e2_" + n, shape, dt))

        rows, rowsT, we, y = sb("rows", [P, R, P]), sb("rowsT", [P, R, P]), sb("we", [P, R, 4, P]), sb("y", [P, R, P])
        pt = ctx.enter_context(nc.psum_tensor("e2_pt", [P, 4, S], F32))
        py = ctx.enter_context(nc.psum_tensor("e2_py", [P, 4, S], F32))
        got = [Signal(ctx, nc, f"e2_got{r}", 32) for r in range(R)]
        stored = [Signal(ctx, nc, f"e2_stored{r}", 16) for r in range(R)]
        turned, copied, product, out = (Signal(ctx, nc, "e2_" + n, R) for n in ("turned", "copied", "product", "out"))
        block = ctx.enter_context(nc.Block())

        def rounds(eng, body):
            body(0)
            body(1)
            with eng.Fori(2, C // R) as i:
                body(i)

        @block.sync
        def _(sp):
            def body(i):
                for r in range(R):
                    product.wait(sp, i - 1, r + 1)
                    sp.dma_start(rows[:, r], net.buf[bass.ds((i * R + r) * P, P)]).then_inc(got[r].sem, 16)
                    sp.dma_start(we[:, r], d["f2_we"][bass.ds((i * R + r) * 4, 4)].rearrange("e p n -> p e n")).then_inc(got[r].sem, 16)
            rounds(sp, body)

        @block.tensor
        def _(pe):
            def turn(i, r):
                got[r].wait(pe, i, 32)
                copied.wait(pe, i - 1, r + 1)
                nc.tensor.transpose(pt[:, r, 0:P], rows[:, r], net.ident[:]).then_inc(turned.sem, 1)

            def body(i):
                for r in range(R):
                    turn(i, r)
                for r in range(R):
                    copied.wait(pe, i, r + 1)
                    out.wait(pe, i - 1, r + 1)
                    for e in range(4):
                        mm = nc.tensor.matmul(py[32 * e:32 * e + 32, r, 0:P], rowsT[:, r, 32 * e:32 * e + 32], we[:, r, e],
                                              start=True, stop=True, tile_position=(0, 32 * e))
                    mm.then_inc(product.sem, 1)
            rounds(pe, body)

        @block.vector
        def _(dve):
            def body(i):
                for r in range(R):
                    turned.wait(dve, i, r + 1)
                    product.wait(dve, i - 1, r + 1)
                    nc.vector.tensor_copy(rowsT[:, r], pt[:, r, 0:P]).then_inc(copied.sem, 1)
            rounds(dve, body)

        @block.scalar
        def _(act):
            def body(i):
                for r in range(R):
                    product.wait(act, i, r + 1)
                    stored[r].wait(act, i - 1, 16)
                    nc.scalar.activation(y[:, r], py[:, r, 0:P], ACT.Copy).then_inc(out.sem, 1)
                    out.wait(act, i, r + 1)
                    act.dma_start(net.ybuf[bass.ds((i * R + r) * P, P)], y[:, r]).then_inc(stored[r].sem, 16)
            rounds(act, body)
            for r in range(R):
                act.wait_ge(stored[r].sem, 16 * (C // R))


def combine_phase(net):
    nc, X = net.nc, net.X
    R = 4
    with ExitStack() as ctx:
        g = ctx.enter_context(nc.sbuf_tensor("c2_g", [P, R, 2, P], F32))
        y = ctx.enter_context(nc.sbuf_tensor("c2_y", [P, R, P], F32))
        pt = ctx.enter_context(nc.psum_tensor("c2_pt", [P, 2, S], F32))
        zeroed, first, mixed, turned, added = (nc.alloc_semaphore("c2_" + n) for n in
                                               ("zeroed", "first", "mixed", "turned", "added"))
        got = [nc.alloc_semaphore(f"c2_got{r}") for r in range(R)]
        block = ctx.enter_context(nc.Block())

        @block.gpsimd
        def _(pool):
            pool.wait_ge(zeroed, 1)
            for n in range(TT):
                if n >= R:
                    pool.wait_ge(mixed, n - R + 1)
                for c in range(2):
                    nc.gpsimd.indirect_dma_start(
                        out=g[:, n % R, c], out_offset=None, in_=net.ybuf,
                        in_offset=bass.IndirectOffsetOnAxis(ap=net.slot[:, c, n:n + 1], axis=0),
                        bounds_check=E128 * CAP - 1, oob_is_err=False).then_inc(got[n % R], 16)

        @block.vector
        def _(dve):
            nc.vector.memset(g[:], 0.0).then_inc(zeroed, 1)

            def mix(n):
                dve.wait_ge(got[n % R], 32 * (n // R + 1))
                if n >= R:
                    dve.wait_ge(turned, n - R + 1)
                nc.vector.tensor_scalar(y[:, n % R], g[:, n % R, 0], net.wgt[:, 0, n:n + 1], None, ALU.mult).then_inc(first, 1)
                dve.wait_ge(first, n + 1)
                nc.vector.scalar_tensor_tensor(y[:, n % R], g[:, n % R, 1], net.wgt[:, 1, n:n + 1], y[:, n % R],
                                               ALU.mult, ALU.add).then_inc(mixed, 1)

            def add(n):
                dve.wait_ge(turned, n + 1)
                x = X[:, n // NT, (n % NT) * P:(n % NT + 1) * P]
                b = n // NT
                nc.vector.scalar_tensor_tensor(x, pt[:, n % 2, 0:P], net.MOD[:, 2, 5, b:b + 1], x, ALU.mult, ALU.add).then_inc(added, 1)
            for n in range(TT):
                mix(n)
                if n:
                    add(n - 1)
            add(TT - 1)

        @block.tensor
        def _(pe):
            for n in range(TT):
                pe.wait_ge(mixed, n + 1)
                if n >= 2:
                    pe.wait_ge(added, n - 1)
                nc.tensor.transpose(pt[:, n % 2, 0:P], y[:, n % R], net.ident[:]).then_inc(turned, 1)


def route_tokens_phase(net):
    nc, d, H = net.nc, net.d, net.H
    with ExitStack() as ctx:
        def sb(n, shape, dt=F32):
            return ctx.enter_context(nc.sbuf_tensor("r3_" + n, shape, dt))

        def sem(n):
            return nc.alloc_semaphore("r3_" + n)

        wr = sb("wr", [P, E8])
        iota = sb("iota", [P, E8])
        lg, p, best = sb("lg", [P, TT, E8]), sb("p", [P, TT, E8]), sb("best", [P, TT, E8])
        index = sb("index", [P, TT, E8], U32)
        mx, ssum = sb("mx", [P, TT]), sb("ssum", [P, TT])
        pair = sb("pair", [P, TT, 2])
        idxf = sb("idxf", [P, 2, TT])
        hot = sb("hot", [P, 2, TT, E8])
        gT = sb("gT", [P, 4, P])
        ps = ctx.enter_context(nc.psum_tensor("r3_ps", [P, TT, E8], F32))
        pt = ctx.enter_context(nc.psum_tensor("r3_pt", [P, 4, P], F32))
        loaded, logit, less_max, exped, gates, turned, copied, stored, ch = (sem(n) for n in (
            "loaded", "logit", "less_max", "exped", "gates", "turned", "copied", "stored", "chain"))
        block = ctx.enter_context(nc.Block())

        @block.sync
        def _(sp):
            sp.dma_start(wr[:], d["f3_wr"]).then_inc(loaded, 16)
            sp.dma_start(iota[:], d["k_route"][1, :, 0:E8]).then_inc(loaded, 16)
            sp.wait_ge(copied, 1)
            for b in range(B):
                sp.dma_start(net.gate_dram[b].rearrange("e (t n) -> t e n", t=NT),
                             gT[32 * (b % 4):32 * (b % 4) + 32, b // 4]).then_inc(stored, 16)
            sp.wait_ge(stored, 16 * B)

        @block.tensor
        def _(pe):
            pe.wait_ge(loaded, 32)
            for n in range(TT):
                mm = nc.tensor.matmul(ps[:, n], H[:, n // NT, (n % NT) * P:(n % NT + 1) * P], wr[:], start=True, stop=True)
            mm.then_inc(logit, 1)
            pe.wait_ge(gates, 1)
            flat = hot[:, 0].rearrange("p n e -> p (n e)")
            for c in range(4):
                tr = nc.tensor.transpose(pt[:, c], flat[:, c * P:(c + 1) * P], net.ident[:])
            tr.then_inc(turned, 1)

        @block.scalar
        def _(act):
            act.wait_ge(less_max, 1)
            nc.scalar.activation(p[:], p[:], ACT.Exp).then_inc(exped, 1)

        @block.vector
        def _(dve):
            k = [0]

            def link(ins):
                k[0] += 1
                ins.then_inc(ch, 1)
                dve.wait_ge(ch, k[0])

            def wait_exp():
                dve.sem_inc(less_max, 1)
                dve.wait_ge(exped, 1)

            dve.wait_ge(logit, 1)
            link(nc.vector.tensor_copy(lg[:], ps[:]))
            softmax_top2(nc, dve, link, wait_exp, lg[:], mx[:], p[:], ssum[:], best[:], index[:], pair[:], TT)
            for c in range(2):
                link(nc.vector.tensor_copy(idxf[:, c], index[:, :, c]))
                link(nc.vector.tensor_tensor(hot[:, c], iota[:].unsqueeze(1).broadcast_to([P, TT, E8]), bcast(idxf[:, c], E8), ALU.is_equal))
                link(nc.vector.tensor_tensor(hot[:, c], hot[:, c], bcast(pair[:, :, c], E8), ALU.mult))
            nc.vector.tensor_tensor(hot[:, 0], hot[:, 0], hot[:, 1], ALU.add).then_inc(gates, 1)
            dve.wait_ge(turned, 1)
            nc.vector.tensor_copy(gT[:], pt[:]).then_inc(copied, 1)


H8, DH64 = 8, 64
INNER = H8 * DH64
WINDOW = 64
PAIRS = INNER // P
GLU = 3


def local_attention_phase(net, name, l):
    nc, H, d = net.nc, net.H, net.d
    UN = NT * PAIRS
    with ExitStack() as ctx:
        def sb(n, shape, dt=F32):
            return ctx.enter_context(nc.sbuf_tensor(name + n, shape, dt))

        def psum(n, shape):
            return ctx.enter_context(nc.psum_tensor(name + n, shape, F32))

        def sig(n, per, credit=0):
            return Signal(ctx, nc, name + n, per, credit)

        w = sb("w", [P, 3, INNER])
        wo = sb("wo", [P, PAIRS, P])
        tab = sb("tab", [P, 2, 2, NT, DH64])
        lens = sb("lens", [P, 2, 2, DH64])
        band = sb("band", [P, 2, 192], BF16)
        bandf = sb("bandf", [P, 192])
        hs = sb("hs", [P, S])
        qk = sb("qk", [P, NT, 2, H8, DH64])
        rot = sb("rot", [P, 2, H8, DH64])
        sq = sb("sq", [P, 2, H8, DH64])
        ss = sb("ss", [P, NT, 2 * H8])
        v = sb("v", [P, 2, NT, INNER])
        qT = sb("qT", [P, 2, PAIRS, S])
        kz = sb("kz", [P, 2, H8, S])
        neg = sb("neg", [P, 4, 2])
        total = sb("total", [P, 4, 2])
        inv = sb("inv", [P, 4, 2])
        prob = sb("prob", [P, 4, 2, 2 * P])
        pt = sb("pt", [P, 2, 2, 2, P])
        c = sb("c", [P, PAIRS, S])
        PJ = psum("PJ", [P, 2, S])
        PV = psum("PV", [P, S])
        PA = psum("PA", [P, 2, 2, 2 * P])
        PT = psum("PT", [P, 2, 4, P])
        PO = psum("PO", [P, PAIRS, P])

        loaded = nc.alloc_semaphore(name + "loaded")
        filled = nc.alloc_semaphore(name + "filled")
        lens_in = nc.alloc_semaphore(name + "lens_in")
        hs_ready = sig("hs_ready", 2)
        projected = sig("projected", 2 * NT)
        squared = sig("squared", NT)
        summed = sig("summed", NT)
        turned = sig("turned", 3 * NT)
        joined = sig("joined", NT)
        v_out = sig("v_out", NT)
        rooted = sig("rooted", 1)
        inverse = sig("inverse", 2)
        scaled = sig("scaled", NT)
        q_turned = sig("q_turned", NT)
        k_turned = sig("k_turned", NT)
        q_here = sig("q_here", NT)
        k_here = sig("k_here", 2 * NT)
        scored = sig("scored", UN)
        maxed = sig("maxed", UN)
        exped = sig("exped", 2 * UN)
        inverted = sig("inverted", UN)
        normed = sig("normed", UN)
        p_turned = sig("p_turned", UN)
        p_here = sig("p_here", UN)
        pv_done = sig("pv_done", UN)
        c_out = sig("c_out", NT)
        y_done = sig("y_done", 1)
        h_added = sig("h_added", 1)
        block = ctx.enter_context(nc.Block())

        def has(b):
            return not isinstance(b, int) or 0 <= b < B

        def steps(eng, step):
            for i in (-1, 0, 1):
                step(i, i % 2)
            with eng.Fori(1, B // 2 - 1) as pair:
                step(pair * 2, 0)
                step(pair * 2 + 1, 1)
            for i in range(B - 2, B + 1):
                step(i, i % 2)

        RC, TR, CT = 1, 3, 4
        SLOTS = UN + CT
        FRONT = {2: 0, 4: 1, 6: 2, 8: 3}
        FRONT2 = {s + 1: t for s, t in FRONT.items()}
        LENGTHS = 10
        SCALE = {10: 0, 11: 1, 13: 2, 15: 3}
        Q_TURN = {12: 0, 14: 1, 16: 2, 18: 3}
        K_TURN = {13: 0, 15: 1, 17: 2, 19: 3}

        @block.sync
        def _(sp):
            sp.dma_start(w[:], d["f1_wqkv"][l].rearrange("j p n -> p j n")).then_inc(loaded, 16)
            sp.dma_start(tab[:], d["f1_tab"].rearrange("a j t p n -> p a j t n")).then_inc(loaded, 16)
            sp.dma_start(lens[:].rearrange("p a j n -> p (a j n)"),
                         d["f1_scale"][l].partition_broadcast(P)).then_inc(loaded, 16)
            sp.dma_start(bandf[:], d["f1_band"]).then_inc(loaded, 16)
            sp.dma_start(wo[:], d["f1_wo"][l].rearrange("(j p) n -> p j n", p=P)).then_inc(loaded, 16)

        @block.tensor
        def _(pe):
            pe.wait_ge(loaded, 80)
            pe.wait_ge(filled, 9)
            ident = net.ident[:]

            def front(b, t):
                hs_ready.wait(pe, b, 2)
                squared.wait(pe, b, t)
                turned.wait(pe, b, 3 * t)
                ht = hs[:, t * P:(t + 1) * P]
                nc.tensor.matmul(PJ[:, 0], ht, w[:, 0], start=True, stop=True)
                nc.tensor.matmul(PJ[:, 1], ht, w[:, 1], start=True, stop=True).then_inc(projected.sem, 1)

            def front2(b, t):
                ht = hs[:, t * P:(t + 1) * P]
                v_out.wait(pe, b, t)
                h_added.wait(pe, b - 2, 1)
                nc.tensor.matmul(PV[:], ht, w[:, 2], start=True, stop=True).then_inc(projected.sem, 1)

            def scores(b, par, u):
                t, hp = divmod(u, PAIRS)
                exped.wait(pe, b, 2 * (u - 1))
                q_here.wait(pe, b, NT)
                k_here.wait(pe, b, 2 * NT)
                k0 = max(0, t * P - WINDOW)
                c0 = k0 - (t - 1) * P
                nc.tensor.matmul(PA[:, u % 2, :, c0:], net.ident_b[:], band[:, :, c0 - WINDOW:], start=True, stop=False)
                for e in range(2):
                    mm = nc.tensor.matmul(PA[:, u % 2, e, c0:], qT[:, par, hp, t * P:(t + 1) * P],
                                          kz[:, par, 2 * hp + e, k0:(t + 1) * P], start=False, stop=(e == 1))
                mm.then_inc(scored.sem, 1)

            def turn_probs(b, u, has_next):
                t = u // PAIRS
                normed.wait(pe, b, u + 1)
                p_here.wait(pe, b, u - 1)
                if has_next:
                    for slots, here, per in ((Q_TURN, q_here, 1), (K_TURN, k_here, 2)):
                        if u + TR - 1 in slots:
                            here.wait(pe, b + 1, per * (slots[u + TR - 1] + 1))
                for e in range(2):
                    for kt in range(0 if t else 1, 2):
                        tr = nc.tensor.transpose(PT[:, u % 2, 2 * e + kt], prob[:, u % 4, e, kt * P:(kt + 1) * P], ident)
                tr.then_inc(p_turned.sem, 1)

            def context(b, par, u):
                t, hp = divmod(u, PAIRS)
                p_here.wait(pe, b, u + 1)
                v_out.wait(pe, b, NT)
                c_out.wait(pe, b, t)
                for kt in range(0 if t else 1, 2):
                    for e in range(2):
                        h = 2 * hp + e
                        mm = nc.tensor.matmul(PO[e * DH64:(e + 1) * DH64, hp], v[:, par, t - 1 + kt, h * DH64:(h + 1) * DH64],
                                              pt[:, u % 2, e, kt], start=(kt == 0 or t == 0), stop=(kt == 1),
                                              tile_position=(0, e * DH64))
                mm.then_inc(pv_done.sem, 1)

            def turn(b, t, side, done):
                for hp in range(PAIRS):
                    tr = nc.tensor.transpose(PT[:, side, hp], qk[:, t, side, 2 * hp:2 * hp + 2].rearrange("p e n -> p (e n)"), ident)
                tr.then_inc(done.sem, 1)

            def step(i, par):
                for s in range(SLOTS):
                    if has(i):
                        if s < UN:
                            scores(i, par, s)
                    if s in FRONT and has(i + 1):
                        front(i + 1, FRONT[s])
                    if has(i):
                        if TR <= s < UN + TR:
                            turn_probs(i, s - TR, has(i + 1))
                        if s >= CT:
                            context(i, par, s - CT)
                    if s == 0 and has(i - 1):
                        c_out.wait(pe, i - 1, NT)
                        if has(i):
                            v_out.wait(pe, i, NT)
                        for j in range(PAIRS):
                            mm = nc.tensor.matmul(PV[:], wo[:, j], c[:, j], start=(j == 0), stop=(j == PAIRS - 1))
                        mm.then_inc(y_done.sem, 1)
                    if has(i + 1):
                        if s in FRONT2:
                            front2(i + 1, FRONT2[s])
                        if s in Q_TURN:
                            t = Q_TURN[s]
                            scaled.wait(pe, i + 1, t + 1)
                            q_here.wait(pe, i + 1, t)
                            if has(i):
                                p_here.wait(pe, i, s - TR)
                            turn(i + 1, t, 0, q_turned)
                        if s in K_TURN:
                            t = K_TURN[s]
                            k_here.wait(pe, i + 1, 2 * t)
                            if has(i):
                                p_here.wait(pe, i, min(s - TR, UN))
                            turn(i + 1, t, 1, k_turned)

            steps(pe, step)

        @block.scalar
        def _(act):
            def shift(b):
                projected.wait(act, b - 1, 2 * NT)
                nc.scalar.activation(hs[0:64], H[0:64, b], ACT.Copy).then_inc(hs_ready.sem, 1)
                nc.scalar.activation(hs[64:P, 1:S], H[64:P, b, 0:S - 1], ACT.Copy).then_inc(hs_ready.sem, 1)

            def front(b, par, t):
                projected.wait(act, b, 2 * t + 1)
                summed.wait(act, b, t)
                nc.scalar.activation(sq[:].rearrange("p a h n -> p a (h n)"), PJ[:], ACT.Square).then_inc(squared.sem, 1)

            def front2(b, par, t):
                projected.wait(act, b, 2 * t + 2)
                pv_done.wait(act, b - 2, UN)
                nc.scalar.activation(v[:, par, t], PV[:], ACT.Copy).then_inc(v_out.sem, 1)

            def exp(b, u):
                c0 = WINDOW if u >= PAIRS else P
                maxed.wait(act, b, u + 1)
                p_turned.wait(act, b, u - 3)
                for e in range(2):
                    nc.scalar.activation(prob[:, u % 4, e, c0:], PA[:, u % 2, e, c0:], ACT.Exp, bias=neg[:, u % 4, e:e + 1],
                                         accum_out=total[:, u % 4, e:e + 1]).then_inc(exped.sem, 1)

            def probs_out(b, u):
                k0 = 0 if u >= PAIRS else 1
                p_turned.wait(act, b, u + 1)
                pv_done.wait(act, b, u - 1)
                nc.scalar.activation(pt[:, u % 2, :, k0:], PT[:, u % 2].rearrange("p (e k) n -> p e k n", e=2)[:, :, k0:],
                                     ACT.Copy).then_inc(p_here.sem, 1)

            def step(i, par):
                if has(i + 1):
                    shift(i + 1)
                for s in range(SLOTS):
                    if has(i):
                        if s < UN:
                            exp(i, s)
                    if s in FRONT and has(i + 1):
                        front(i + 1, 1 - par, FRONT[s])
                    if has(i):
                        if TR <= s < UN + TR:
                            probs_out(i, s - TR)
                    if has(i + 1):
                        b = i + 1
                        if s in FRONT2:
                            front2(b, 1 - par, FRONT2[s])
                        if s == LENGTHS:
                            summed.wait(act, b, NT)
                            nc.scalar.activation(ss[:], ss[:], ACT.Sqrt).then_inc(rooted.sem, 1)
                        if s in K_TURN:
                            t = K_TURN[s]
                            k_turned.wait(act, b, t + 1)
                            scored.wait(act, b - 2, UN)
                            for e in range(2):
                                rows = slice(e * DH64, (e + 1) * DH64)
                                nc.scalar.activation(kz[rows, 1 - par, e::2, t * P:(t + 1) * P], PT[rows, 1], ACT.Copy
                                                     ).then_inc(k_here.sem, 1)

            steps(act, step)

        @block.gpsimd
        def _(pool):
            nc.gpsimd.memset(kz[:], 0.0).then_inc(filled, 1)
            nc.gpsimd.memset(prob[:], 0.0).then_inc(filled, 1)
            pool.wait_ge(filled, 9)

            def step(i, par):
                for s in range(SLOTS):
                    u = s - RC
                    if has(i) and 0 <= u < UN:
                        inverted.wait(pool, i, u + 1)
                        c0 = WINDOW if u >= PAIRS else P
                        pr = prob[:, u % 4, :, c0:]
                        nc.gpsimd.tensor_tensor(pr, pr, inv[:, u % 4].unsqueeze(2).broadcast_to([P, 2, 2 * P - c0]),
                                                ALU.mult).then_inc(normed.sem, 1)
                    if has(i + 1):
                        b = i + 1
                        if s in FRONT2:
                            t = FRONT2[s]
                            turned.wait(pool, b, 3 * t + 3)
                            nc.gpsimd.tensor_tensor(qk[:, t], qk[:, t], rot[:], ALU.add).then_inc(joined.sem, 1)
                        if s in SCALE:
                            t = SCALE[s]
                            inverse.wait(pool, b, 2)
                            joined.wait(pool, b, t + 1)
                            x = qk[:, t].rearrange("p a h n -> p (a h) n")
                            nc.gpsimd.tensor_tensor(x, x, ss[:, t].unsqueeze(2).broadcast_to([P, 2 * H8, DH64]),
                                                    ALU.mult).then_inc(scaled.sem, 1)

            steps(pool, step)

        @block.vector
        def _(dve):
            nc.vector.memset(hs[64:P, 0:1], 0.0).then_inc(filled, 1)
            dve.wait_ge(loaded, 80)
            for a in range(2):
                for j in range(2):
                    nc.vector.tensor_tensor(tab[:, a, j], tab[:, a, j], lens[:, a, j].unsqueeze(1).broadcast_to([P, NT, DH64]),
                                            ALU.mult).then_inc(filled, 1)
            for e in range(2):
                nc.vector.tensor_copy(band[:, e], bandf[:]).then_inc(filled, 1)
            dve.wait_ge(filled, 9)

            lo, hi = slice(0, DH64 // 2), slice(DH64 // 2, DH64)
            x = PJ[:].rearrange("p a (h n) -> p a h n", n=DH64)

            def table(a, t):
                return tab[:, a, :, t].unsqueeze(2).broadcast_to([P, 2, H8, DH64])

            def front(b, t):
                squared.wait(dve, b, t + 1)
                scaled.wait(dve, b - 1, NT)
                k_turned.wait(dve, b - 1, NT)
                joined.wait(dve, b, t)
                nc.vector.tensor_tensor(qk[:, t], x, table(0, t), ALU.mult).then_inc(turned.sem, 1)
                nc.vector.tensor_tensor(rot[:, :, :, lo], x[:, :, :, hi], table(1, t)[:, :, :, lo], ALU.mult).then_inc(turned.sem, 1)

            def front2(b, t):
                nc.vector.tensor_tensor(rot[:, :, :, hi], x[:, :, :, lo], table(1, t)[:, :, :, hi], ALU.mult).then_inc(turned.sem, 1)
                nc.vector.tensor_reduce(ss[:, t], sq[:].rearrange("p a h n -> p (a h) n"), AX, ALU.add).then_inc(summed.sem, 1)

            def step(i, par):
                for s in range(SLOTS):
                    if s in FRONT2 and has(i + 1):
                        front(i + 1, FRONT2[s])
                    if has(i):
                        if s < UN:
                            c0 = WINDOW if s >= PAIRS else P
                            scored.wait(dve, i, s + 1)
                            nc.vector.tensor_reduce(neg[:, s % 4], PA[:, s % 2, :, c0:], AX, ALU.max, negate=True
                                                    ).then_inc(maxed.sem, 1)
                        u = s - RC
                        if 0 <= u < UN:
                            exped.wait(dve, i, 2 * u + 2)
                            nc.vector.reciprocal(inv[:, u % 4], total[:, u % 4]).then_inc(inverted.sem, 1)
                        if s >= CT and (s - CT) % PAIRS == PAIRS - 1:
                            t = (s - CT) // PAIRS
                            pv_done.wait(dve, i, PAIRS * (t + 1))
                            y_done.wait(dve, i - 1, 1)
                            nc.vector.tensor_copy(c[:, :, t * P:(t + 1) * P], PO[:]).then_inc(c_out.sem, 1)
                    if s == 1 and has(i - 1):
                        y_done.wait(dve, i - 1, 1)
                        nc.vector.tensor_tensor(H[:, i - 1], PV[:], H[:, i - 1], ALU.add).then_inc(h_added.sem, 1)
                    if has(i + 1):
                        b = i + 1
                        if s in FRONT2:
                            front2(b, FRONT2[s])
                        if s == LENGTHS:
                            rooted.wait(dve, b, 1)
                            nc.vector.tensor_scalar(ss[:], ss[:], 1e-12, None, ALU.max).then_inc(inverse.sem, 1)
                            inverse.wait(dve, b, 1)
                            nc.vector.reciprocal(ss[:], ss[:]).then_inc(inverse.sem, 1)
                        if s in Q_TURN:
                            t = Q_TURN[s]
                            q_turned.wait(dve, b, t + 1)
                            scored.wait(dve, b - 2, UN)
                            nc.vector.tensor_copy(qT[:, 1 - par, :, t * P:(t + 1) * P], PT[:, 0]).then_inc(q_here.sem, 1)

            steps(dve, step)


def glu_phase(net, name, l, last):
    nc, X, H, N, d = net.nc, net.X, net.H, net.N, net.d
    gate = net.MOD[:, 1, 5]
    with ExitStack() as ctx:
        def sb(n, shape, dt=F32):
            return ctx.enter_context(nc.sbuf_tensor(name + n, shape, dt))

        w1 = sb("w1", [P, 2 * GLU, P])
        w2 = sb("w2", [P, GLU, P])
        b1 = sb("b1", [P, 2 * GLU])
        b2 = sb("b2", [P, 1])
        g = sb("g", [P, 2, GLU, S])
        pa = ctx.enter_context(nc.psum_tensor(name + "pa", [P, 3, S], F32))
        pg = ctx.enter_context(nc.psum_tensor(name + "pg", [P, 3, S], F32))
        po = ctx.enter_context(nc.psum_tensor(name + "po", [P, 2, S], F32))
        loaded = nc.alloc_semaphore(name + "loaded")
        up_g = Signal(ctx, nc, name + "up_g", GLU)
        up_a = Signal(ctx, nc, name + "up_a", GLU)
        gelued = Signal(ctx, nc, name + "gelued", GLU)
        gated = Signal(ctx, nc, name + "gated", GLU)
        down_done = Signal(ctx, nc, name + "down", 1)
        added = Signal(ctx, nc, name + "added", 1)
        x_done = Signal(ctx, nc, name + "x_done", 1)
        block = ctx.enter_context(nc.Block())

        def batches(eng, batch):
            for b in range(4):
                batch(b, b % 2)
            with eng.Fori(2, B // 2) as pair:
                batch(pair * 2, 0)
                batch(pair * 2 + 1, 1)

        @block.sync
        def _(sp):
            sp.dma_start(w1[:], d["f1_w1"][l].rearrange("p (j n) -> p j n", n=P)).then_inc(loaded, 16)
            sp.dma_start(w2[:], d["f1_w2"][l].rearrange("(j p) n -> p j n", p=P)).then_inc(loaded, 16)
            sp.dma_start(b1[:], d["f1_b1"][l]).then_inc(loaded, 16)
            sp.dma_start(b2[:], d["f1_b2"][l]).then_inc(loaded, 16)

        @block.tensor
        def _(pe):
            pe.wait_ge(loaded, 64)

            def down(b, par):
                gated.wait(pe, b, GLU)
                added.wait(pe, b - 2, 1)
                for j in range(GLU):
                    mm = nc.tensor.matmul(po[:, par], w2[:, j], g[:, par, j], start=(j == 0), stop=(j == GLU - 1))
                mm.then_inc(down_done.sem, 1)

            def batch(b, par):
                for j in range(GLU):
                    gelued.wait(pe, b - 1, j + 1)
                    nc.tensor.matmul(pg[:, j], w1[:, GLU + j], N[:, b], start=True, stop=True).then_inc(up_g.sem, 1)
                    gated.wait(pe, b - 1, j + 1)
                    nc.tensor.matmul(pa[:, j], w1[:, j], N[:, b], start=True, stop=True).then_inc(up_a.sem, 1)
                if not (isinstance(b, int) and b == 0):
                    down(b - 1, 1 - par)
            batches(pe, batch)
            down(B - 1, 1)

        @block.scalar
        def _(act):
            act.wait_ge(loaded, 64)

            def batch(b, par):
                down_done.wait(act, b - 2, 1)
                for j in range(GLU):
                    up_g.wait(act, b, j + 1)
                    nc.scalar.activation(g[:, par, j], pg[:, j], ACT.Gelu, bias=b1[:, GLU + j:GLU + j + 1]).then_inc(gelued.sem, 1)
            batches(act, batch)

        @block.vector
        def _(dve):
            dve.wait_ge(loaded, 64)

            def add(b, par):
                down_done.wait(dve, b, 1)
                h = H[:, b]
                nc.vector.scalar_tensor_tensor(h, po[:, par], b2[:, 0:1], h, ALU.add, ALU.add).then_inc(added.sem, 1)
                if last:
                    added.wait(dve, b, 1)
                    nc.vector.scalar_tensor_tensor(X[:, b], h, col(gate, b), X[:, b], ALU.mult, ALU.add).then_inc(x_done.sem, 1)

            def batch(b, par):
                for j in range(GLU):
                    up_a.wait(dve, b, j + 1)
                    gelued.wait(dve, b, j + 1)
                    x = g[:, par, j]
                    nc.vector.scalar_tensor_tensor(x, pa[:, j], b1[:, j:j + 1], x, ALU.add, ALU.mult).then_inc(gated.sem, 1)
                if not (isinstance(b, int) and b == 0):
                    add(b - 1, 1 - par)
            batches(dve, batch)
            add(B - 1, 1)


def small_transformer_phases(net):
    nc = net.nc
    with ExitStack() as ctx:
        net.split_center = ctx.enter_context(nc.sbuf_tensor("split_center", [P, 2, P], F32))
        net.ln = ctx.enter_context(nc.sbuf_tensor("f1_ln", [P, 2, 2], F32))
        with nc.cleanup_on_exit(), nc.Block() as block:
            loaded = nc.alloc_semaphore("f1_shared_loaded")

            @block.sync
            def _(sp):
                sp.dma_start(net.split_center[:], net.d["k_split_center"].rearrange("a p n -> p a n")).then_inc(loaded, 16)
                sp.dma_start(net.ln[:], net.d["f1_ln"]).then_inc(loaded, 16)
                sp.wait_ge(loaded, 32)
        for l in range(2):
            with nc.cleanup_on_exit():
                local_attention_phase(net, f"f1a{l}_", l)
            with nc.sbuf_tensor(f"N{l}", [P, B, S], F32) as net.N:
                with nc.cleanup_on_exit():
                    norm_phase(net, f"f1n{l}_", 1, 1, small=l)
                with nc.cleanup_on_exit():
                    glu_phase(net, f"f1g{l}_", l, last=(l == 1))


def more_layouts(a, out):
    f4 = lambda v: v.reshape(-1, F4, P).transpose(0, 2, 1)
    out["f0_wg"], out["f0_bg"] = a["L0_ffn_w_gate"], a["L0_ffn_b_gate"]
    out["f0_alpha"] = a["L0_ffn_alpha"].reshape(1)
    out["f0_w1m"], out["f0_w2m"] = a["L0_ffn_W1m"], a["L0_ffn_W2m"]
    out["f0_bm"] = np.concatenate([f4(a["L0_ffn_b1m"])[0], a["L0_ffn_b2m"][:, None]], 1)
    out["f0_w1e"], out["f0_w2e"] = a["L0_ffn_W1e"], a["L0_ffn_W2e"]
    out["f0_be"] = np.concatenate([f4(a["L0_ffn_b1e"]), a["L0_ffn_b2e"][:, :, None]], 2)
    join = lambda s, e: np.concatenate([a["L3_ffn_" + s][None], a["L3_ffn_" + e]])
    out["f3_w1"], out["f3_w2"] = join("Wfc_s", "Wfc"), join("Wproj_s", "Wproj")
    out["f3_b"] = np.concatenate([f4(join("bfc_s", "bfc")), join("bproj_s", "bproj")[:, :, None]], 2)
    out["a2_w"] = np.stack([a["L2_attn_W" + c] for c in "qkvo"])
    out["f2_wg"], out["f2_we"] = a["L2_ffn_wg"], a["L2_ffn_we"]
    out["f1_wqkv"] = a["L1_ffn_wqkv"].reshape(2, P, 3, INNER).transpose(0, 2, 1, 3)
    out["f1_wo"] = a["L1_ffn_wo"]
    swap = lambda v: np.concatenate([v[:, DH64 // 2:], v[:, :DH64 // 2]], 1)
    qs, ks = a["L1_ffn_q_scale"], a["L1_ffn_k_scale"]
    out["f1_scale"] = np.stack([qs, ks, swap(qs), swap(ks)], 1).reshape(2, 4 * DH64)
    hidden = a["L1_ffn_w2"].shape[1]
    pad = lambda v, axis: np.concatenate([v, np.zeros([GLU * P - hidden if i == axis else n for i, n in enumerate(v.shape)], v.dtype)], axis)
    halves = lambda v, axis: np.concatenate([pad(h, axis) for h in np.split(v, 2, axis)], axis)
    out["f1_w1"], out["f1_w2"] = halves(a["L1_ffn_w1"], 2), pad(a["L1_ffn_w2"], 1)
    out["f1_b1"] = halves(a["L1_ffn_b1"], 1).reshape(2, 2 * GLU, P).transpose(0, 2, 1)
    out["f1_b2"] = a["L1_ffn_b2"][:, :, None]
    out["f1_ln"] = np.stack([a["L1_ffn_ln_g"].T, a["L1_ffn_ln_b"].T], 1)
    out["f3_wr"] = a["L3_ffn_Wr"]


def store_phase(net):
    nc = net.nc
    with ExitStack() as ctx:
        stored = nc.alloc_semaphore("stored")
        block = ctx.enter_context(nc.Block())

        @block.sync
        def _(sp):
            for b in range(0, B, 4):
                sp.dma_start(net.d["out"][:, b:b + 4], net.X[:, b:b + 4]).then_inc(stored, 16)
            sp.wait_ge(stored, 16 * (B // 4))


def build(nc, d):
    net = Net()
    net.nc, net.d = nc, d
    nc.disable_value_cache = True
    with ExitStack() as ctx:
        load_shared(net, ctx)
        net.buf = nc.dram_tensor("slots_in", [E128 * CAP, P], F32, kind="Internal").ap()
        net.ybuf = nc.dram_tensor("slots_out", [E128 * CAP, P], F32, kind="Internal").ap()
        net.gate_dram = nc.dram_tensor("token_gates", [B, E8, S], F32, kind="Internal").ap()
        with nc.cleanup_on_exit():
            modulation_phase(net)
        with nc.cleanup_on_exit():
            norm_phase(net, "n0a_", 0, 0)
        with nc.cleanup_on_exit():
            heads16_phase(net, "a0_", 0, causal=True, rope=True, w_sum=False)
        with nc.cleanup_on_exit():
            norm_phase(net, "n0b_", 0, 1)
        with nc.cleanup_on_exit():
            route_batches_phase(net)
        with nc.cleanup_on_exit():
            mlp_phase(net, "f0_", 0, 3, True)
        with nc.cleanup_on_exit():
            norm_phase(net, "n1a_", 1, 0)
        with nc.cleanup_on_exit():
            heads16_phase(net, "a1_", 1, causal=True, rope=False, w_sum=True)
        with nc.cleanup_on_exit():
            norm_phase(net, "n1b_", 1, 1)
        small_transformer_phases(net)
        with nc.cleanup_on_exit():
            norm_phase(net, "n2a_", 2, 0)
        with nc.cleanup_on_exit():
            wide_head_phase(net, "a2_", 2)
        with nc.cleanup_on_exit():
            norm_phase(net, "n2b_", 2, 1)
        with nc.cleanup_on_exit():
            route_slots_phase(net)
        with nc.cleanup_on_exit():
            dispatch_phase(net)
        with nc.cleanup_on_exit():
            experts_phase(net)
        with nc.cleanup_on_exit():
            combine_phase(net)
        with nc.cleanup_on_exit():
            norm_phase(net, "n3a_", 3, 0)
        with nc.cleanup_on_exit():
            heads16_phase(net, "a3_", 3, causal=False, rope=True, w_sum=False)
        with nc.cleanup_on_exit():
            norm_phase(net, "n3b_", 3, 1)
        with nc.cleanup_on_exit():
            route_tokens_phase(net)
        with nc.cleanup_on_exit():
            mlp_phase(net, "f3_", 3, 9, False)
        with nc.cleanup_on_exit():
            store_phase(net)


def constants():
    f = np.float32
    k = np.arange(P)
    pos = np.arange(S, dtype=f)
    out = {
        "k_ident": np.eye(P, dtype=f),
        "k_center": (np.eye(P) - 1.0 / P).astype(f),
        "k_mean": np.full((P, P), 1.0 / P, f),
        "k_mask": np.stack([np.where(k[None, :] > k[:, None], BIG, 0.0),
                            np.where(k[:, None] > k[None, :], BIG, 0.0)]).astype(f),
    }
    out["k_route"] = np.stack([(k[:, None] < k[None, :]).astype(f), np.tile(k.astype(f), (P, 1))])
    freq = np.power(f(10000.0), f(-2.0) * np.arange(P // 2, dtype=f) / f(P)).astype(f)
    angle = (freq[:, None] * pos[None, :]).astype(f)
    sin, cos = np.sin(angle).astype(f), np.cos(angle).astype(f)
    out["a0_turn"] = np.stack([np.concatenate([cos, sin]), np.concatenate([-sin, -cos])])
    inv = (f(1.0) / np.power(f(10000.0), np.arange(0, DH8, 2, dtype=f) / f(DH8))).astype(f)
    angle = np.repeat((inv[:, None] * pos[None, :]).astype(f), 2, axis=0)
    sign = np.where(np.arange(DH8) < DH8 // 2, -1.0, 1.0).astype(f)[:, None]
    out["a3_turn"] = np.stack([np.tile(np.cos(angle), (H16, 1)), np.tile(np.sin(angle) * sign, (H16, 1))]).astype(f)
    center = (np.eye(P) - 1.0 / P).astype(f)
    first = (k < P // 2)[:, None].astype(f)
    out["k_split_center"] = np.stack([center * first, center * (1 - first)])
    half = np.arange(0, DH64, 2, dtype=f)
    freqs = pos[:, None] * (f(1.0) / f(10000.0) ** (half / f(DH64)))[None, :]
    base = (half + f(0.4 * DH64)) / f(1.4 * DH64)
    stretch = base[None, :] ** ((pos - S // 2) / f(WINDOW // 2))[:, None]
    twice = lambda v: np.concatenate([v, v], 1)
    cos, sin, stretch = twice(np.cos(freqs)), twice(np.sin(freqs)), twice(stretch)
    sin = sin * np.where(np.arange(DH64) < DH64 // 2, -1.0, 1.0).astype(f)
    out["f1_tab"] = np.stack([[v * stretch * f(8.0), v / stretch] for v in (cos, sin)]).astype(f).reshape(2, 2, NT, P, DH64)
    dist = (k[:, None] + WINDOW) - np.arange(WINDOW + P)[None, :]
    out["f1_band"] = np.where((dist < 0) | (dist > WINDOW), BIG, 0.0).astype(f)
    return out


def by_group(w):
    out = np.zeros((G, 4, 32, P), w.dtype)
    out[:, :, :DH8] = w.reshape(G, 4, DH8, P)
    return out.reshape(G, P, P)


def laid_out(x):
    a = {k: np.asarray(v) for k, v in x.items()}
    row = lambda v: np.ascontiguousarray(v).reshape(1, -1)
    colm = lambda v: np.ascontiguousarray(v).reshape(-1, 1)
    out = {
        "xT": a["L0_attn_x"].transpose(2, 0, 1),
        "cT": np.stack([a[f"L{l}_c"].T for l in range(4)]),
        "wmod": np.stack([a[f"L{l}_wmod"] for l in range(4)]),
    }
    even = np.concatenate([np.arange(0, P, 2)] * 2)
    odd = np.concatenate([np.arange(1, P, 2)] * 2)
    swap = (np.arange(P).reshape(H16, 2, DH8 // 2)[:, ::-1]).reshape(-1)
    same = np.arange(P)
    for n, l, t, picks in (("a0_", 0, "L0_attn_W", (even, odd)), ("a3_", 3, "L3_attn_w", (same, swap))):
        w = {c: a[t + c] if l == 0 else a[t + c].T for c in "qkvo"}
        bias = {c: a[f"L{l}_attn_b{c}"] for c in "qkvo"}
        out[n + "wqk"] = np.stack([w[c][:, p] for c in "qk" for p in picks])
        out[n + "bqk"] = np.stack([bias[c][p] for c in "qk" for p in picks], axis=1)
        out[n + "wv"], out[n + "bv"] = w["v"], bias["v"]
        out[n + "wo"], out[n + "bo"] = by_group(w["o"]), colm(bias["o"])
    w = a["L1_attn_W_qkv"].transpose(1, 0, 2).reshape(P, H16, 3, DH8).transpose(2, 0, 1, 3).reshape(3, P, P)
    out["a1_wqk"], out["a1_wv"] = w[0:2], w[2]
    out["a1_wo"] = a["L1_attn_W_out"].reshape(P, P)
    more_layouts(a, out)
    return {k: np.ascontiguousarray(v) for k, v in out.items()}


def kernel(**inputs):
    import concourse.bacc as _bacc
    from concourse.bass_utils import run_bass_kernel_spmd as _run

    nc = _bacc.Bacc("TRN2", target_bir_lowering=False, num_devices=1)
    arrays, aps = {}, {}
    for name, value in {**laid_out(inputs), **constants()}.items():
        arrays["in_" + name] = value
        aps[name] = nc.dram_tensor("in_" + name, value.shape, mybir.dt.from_np(value.dtype), kind="ExternalInput").ap()
    aps["out"] = nc.dram_tensor("out_0_dram", (P, B, S), F32, kind="ExternalOutput").ap()
    build(nc, aps)
    r = _run(nc, [arrays], core_ids=[0])
    return np.ascontiguousarray(np.asarray(r.results[0]["out_0_dram"]).transpose(1, 2, 0))
```
